# Optimizing a Trainium2 kernel written in Bass

```python
import numpy as np
import jax
import jax.numpy as jnp

def _softmax(x, axis=-1):
    return jax.nn.softmax(x, axis=axis)

def _gelu(x):
    return jax.nn.gelu(x, approximate=True)

def _silu(x):
    return jax.nn.silu(x)

def _sigmoid(x):
    return jax.nn.sigmoid(x)

def _layernorm(x, axis=-1, eps=1e-05):
    m = jnp.mean(x, axis=axis, keepdims=True)
    v = jnp.var(x, axis=axis, keepdims=True)
    return (x - m) / jnp.sqrt(v + eps)

def _scatter_add(tgt, idx, src, axis=0):
    return tgt.at[idx].add(src)

def _segment_sum(src, seg, n):
    return jax.ops.segment_sum(src, seg, n)
kernel_name = 'mk_lm_tower_d1_tok_ids1024_r4_b565ba'

def setup_inputs(seed: int=0):
    np.random.seed(seed)
    _w = jnp.asarray

    def _rec_inputs():
        import jax
        import jax.numpy as jnp
        _rk = jax.random.key(seed)
        x = jax.random.randint(jax.random.fold_in(_rk, 1), (8, 512), 0, 12564, jnp.int32)
        return x
    x = _rec_inputs()

    def _L0_tok_setup():
        import jax, jax.numpy as jnp
        import numpy as np
        VOCAB = 50257
        DIM = 256
        R = 16
        ALPHA = 32
        SCALING = ALPHA / R
        key = jax.random.key(seed)
        k1, k2, k3, k4 = jax.random.split(key, 4)
        input_ids = jax.random.randint(k1, (4, 1024), 0, VOCAB)
        emb_weight = jax.random.normal(k2, (VOCAB, DIM), dtype=jnp.float32)
        lora_A = jax.random.normal(k3, (R, VOCAB), dtype=jnp.float32) * (1.0 / R)
        lora_B = jax.random.normal(k4, (DIM, R), dtype=jnp.float32) * 0.02
        return {'input': input_ids, 'emb_weight': emb_weight, 'lora_A': lora_A, 'lora_B': lora_B}
    _L0_tok_all = _L0_tok_setup()
    _L0_tok_in = {k: v for k, v in _L0_tok_all.items() if k in ('emb_weight', 'lora_A', 'lora_B')}
    del _L0_tok_all

    def _L0_attn_setup():
        import jax, jax.numpy as jnp
        import numpy as np
        B, T, D = (2, 512, 256)
        HD = 128
        NH = 16
        NKV = 8
        EPS = 1e-06
        ROPE_THETA = 1000000.0

        def _rms_norm(x, w):
            rms = jnp.sqrt(jnp.mean(x * x, axis=-1, keepdims=True))
            return w * (x / (rms + EPS))

        def _rope_cos_sin(seq_len):
            pos = jnp.arange(seq_len, dtype=jnp.float32)
            thetas = ROPE_THETA ** (-2.0 * jnp.arange(HD // 2, dtype=jnp.float32) / HD)
            freqs = pos[:, None] * thetas[None, :]
            return (jnp.cos(freqs), jnp.sin(freqs))

        def _apply_rope(x, cos, sin):
            xr = x[..., 0::2]
            xi = x[..., 1::2]
            c = cos[None, None, :, :]
            s = sin[None, None, :, :]
            out_r = xr * c - xi * s
            out_i = xr * s + xi * c
            return jnp.stack([out_r, out_i], axis=-1).reshape(x.shape)
        key = jax.random.key(seed)
        ks = jax.random.split(key, 7)
        s = 0.02
        return {'x': jax.random.normal(ks[0], (B, T, D), dtype=jnp.float32), 'wq': jax.random.normal(ks[1], (D, NH * HD), dtype=jnp.float32) * s, 'wk': jax.random.normal(ks[2], (D, NKV * HD), dtype=jnp.float32) * s, 'wv': jax.random.normal(ks[3], (D, NKV * HD), dtype=jnp.float32) * s, 'wo': jax.random.normal(ks[4], (NH * HD, D), dtype=jnp.float32) * s, 'q_norm_w': jnp.ones((HD,), dtype=jnp.float32), 'k_norm_w': jnp.ones((HD,), dtype=jnp.float32)}
    _L0_attn_all = _L0_attn_setup()
    _L0_attn_in = {k: v for k, v in _L0_attn_all.items() if k in ('wq', 'wk', 'wv', 'wo', 'q_norm_w', 'k_norm_w')}
    del _L0_attn_all

    def _L0_ffn_setup():
        import jax, jax.numpy as jnp
        import numpy as np
        NUM_EXPERTS = 8
        TOP_K = 2
        N_EMBD = 256
        B, T = (4, 512)
        key = jax.random.key(seed)
        k_x, k_g, k_e = jax.random.split(key, 3)
        x = jax.random.normal(k_x, (B, T, N_EMBD), dtype=jnp.float32)
        scale = 1.0 / np.sqrt(N_EMBD)
        gate_w = jax.random.uniform(k_g, (NUM_EXPERTS, N_EMBD), dtype=jnp.float32, minval=-scale, maxval=scale)
        expert_w = jax.random.uniform(k_e, (NUM_EXPERTS, N_EMBD, N_EMBD), dtype=jnp.float32, minval=-scale, maxval=scale)
        return {'x': x, 'gate_w': gate_w, 'expert_w': expert_w}
    _L0_ffn_all = _L0_ffn_setup()
    _L0_ffn_in = {k: v for k, v in _L0_ffn_all.items() if k in ('gate_w', 'expert_w')}
    del _L0_ffn_all
    return {'x': x, 'L0_tok_emb_weight': _L0_tok_in['emb_weight'], 'L0_tok_lora_A': _L0_tok_in['lora_A'], 'L0_tok_lora_B': _L0_tok_in['lora_B'], 'L0_attn_wq': _L0_attn_in['wq'], 'L0_attn_wk': _L0_attn_in['wk'], 'L0_attn_wv': _L0_attn_in['wv'], 'L0_attn_wo': _L0_attn_in['wo'], 'L0_attn_q_norm_w': _L0_attn_in['q_norm_w'], 'L0_attn_k_norm_w': _L0_attn_in['k_norm_w'], 'L0_ffn_gate_w': _L0_ffn_in['gate_w'], 'L0_ffn_expert_w': _L0_ffn_in['expert_w']}

def reference(x, L0_tok_emb_weight, L0_tok_lora_A, L0_tok_lora_B, L0_attn_wq, L0_attn_wk, L0_attn_wv, L0_attn_wo, L0_attn_q_norm_w, L0_attn_k_norm_w, L0_ffn_gate_w, L0_ffn_expert_w):
    import jax
    import jax.numpy as jnp

    def _L0_tok_ref(input, emb_weight, lora_A, lora_B):
        import jax, jax.numpy as jnp
        import numpy as np
        VOCAB = 50257
        DIM = 256
        R = 16
        ALPHA = 32
        SCALING = ALPHA / R
        orig_out = jnp.take(emb_weight, input, axis=0)
        a_rows = jnp.take(lora_A, input, axis=1)
        a_rows = jnp.moveaxis(a_rows, 0, -1)
        lora_out = jnp.einsum('bsr,dr->bsd', a_rows, lora_B) * SCALING
        return orig_out + lora_out

    def _L0_attn_ref(x, wq, wk, wv, wo, q_norm_w, k_norm_w):
        import jax, jax.numpy as jnp
        import numpy as np
        B, T, D = (2, 512, 256)
        HD = 128
        NH = 16
        NKV = 8
        EPS = 1e-06
        ROPE_THETA = 1000000.0

        def _rms_norm(x, w):
            rms = jnp.sqrt(jnp.mean(x * x, axis=-1, keepdims=True))
            return w * (x / (rms + EPS))

        def _rope_cos_sin(seq_len):
            pos = jnp.arange(seq_len, dtype=jnp.float32)
            thetas = ROPE_THETA ** (-2.0 * jnp.arange(HD // 2, dtype=jnp.float32) / HD)
            freqs = pos[:, None] * thetas[None, :]
            return (jnp.cos(freqs), jnp.sin(freqs))

        def _apply_rope(x, cos, sin):
            xr = x[..., 0::2]
            xi = x[..., 1::2]
            c = cos[None, None, :, :]
            s = sin[None, None, :, :]
            out_r = xr * c - xi * s
            out_i = xr * s + xi * c
            return jnp.stack([out_r, out_i], axis=-1).reshape(x.shape)
        b, t, d = x.shape
        q = (x @ wq).reshape(b, t, NH, HD).transpose(0, 2, 1, 3)
        k = (x @ wk).reshape(b, t, NKV, HD).transpose(0, 2, 1, 3)
        v = (x @ wv).reshape(b, t, NKV, HD).transpose(0, 2, 1, 3)
        q = _rms_norm(q, q_norm_w)
        k = _rms_norm(k, k_norm_w)
        rep = NH // NKV
        k = jnp.repeat(k, rep, axis=1)
        v = jnp.repeat(v, rep, axis=1)
        cos, sin = _rope_cos_sin(t)
        q = _apply_rope(q, cos, sin)
        k = _apply_rope(k, cos, sin)
        scale = 1.0 / jnp.sqrt(jnp.float32(HD))
        scores = jnp.einsum('bhqd,bhkd->bhqk', q, k) * scale
        mask = jnp.triu(jnp.full((t, t), -jnp.inf, dtype=scores.dtype), k=1)
        scores = scores + mask
        attn = jax.nn.softmax(scores.astype(jnp.float32), axis=-1).astype(q.dtype)
        y = jnp.einsum('bhqk,bhkd->bhqd', attn, v)
        y = y.transpose(0, 2, 1, 3).reshape(b, t, NH * HD)
        return y @ wo

    def _L0_ffn_ref(x, gate_w, expert_w):
        import jax, jax.numpy as jnp
        import numpy as np
        NUM_EXPERTS = 8
        TOP_K = 2
        N_EMBD = 256
        B, T = (4, 512)
        Bb, Tt, C = x.shape
        xf = x.reshape(Bb * Tt, C)
        logits = xf @ gate_w.T
        w, sel = jax.lax.top_k(logits, TOP_K)
        w = jax.nn.softmax(w.astype(jnp.float32), axis=1).astype(xf.dtype)
        n = xf.shape[0]
        w_full = jnp.zeros((n, NUM_EXPERTS), dtype=xf.dtype)
        w_full = w_full.at[jnp.arange(n)[:, None], sel].add(w)
        expert_out = jnp.einsum('nc,edc->ned', xf, expert_w)
        out = jnp.einsum('ne,ned->nd', w_full, expert_out)
        return out.reshape(Bb, Tt, C)
    h = _L0_tok_ref(x, L0_tok_emb_weight, L0_tok_lora_A, L0_tok_lora_B)
    h = h + _L0_attn_ref(_layernorm(h, axis=-1), L0_attn_wq, L0_attn_wk, L0_attn_wv, L0_attn_wo, L0_attn_q_norm_w, L0_attn_k_norm_w)
    h = h + _L0_ffn_ref(_layernorm(h, axis=-1), L0_ffn_gate_w, L0_ffn_expert_w)
    return h

_drawn_inputs = setup_inputs


def setup_inputs(seed=0):
    import zlib

    import numpy as np

    out = dict(_drawn_inputs(seed))
    spreads = {'L0_attn_q_norm_w': (1.0, 0.2), 'L0_attn_k_norm_w': (1.0, 0.2)}
    factors = {}
    for name, (base, spread) in spreads.items():
        noise = np.random.default_rng([zlib.crc32(name.encode()), seed]).standard_normal(out[name].shape)
        drawn = base * np.exp(spread * noise) if base else spread * noise
        out[name] = jnp.asarray(drawn.astype(out[name].dtype))
    for name, factor in factors.items():
        out[name] = (out[name] * factor).astype(out[name].dtype)
    return out
```

```python
from contextlib import ExitStack

import concourse.bass as bass
from concourse import mybir

F32 = mybir.dt.float32
F32R = mybir.dt.float32r
BF16 = mybir.dt.bfloat16
I32 = mybir.dt.int32
U32 = mybir.dt.uint32
ALU = mybir.AluOpType
ACT = mybir.ActivationFunctionType
AX = mybir.AxisListType.X

B, T, D = 8, 512, 256
R = 16
LORA_SCALING = 2.0
HD, NH, NKV = 128, 16, 8
REP = NH // NKV
NE = 8
P = 128
NT = T // P
KC = D // P
U = REP * NT
EPC = 2
NCH = NE // EPC
NS = NKV + NCH
SL = KC * 512
ATT_SCALE = float(HD) ** -0.5
RMS_EPS = 1e-6
LN_EPS = 1e-5


def wait_past(eng, sem, value):
    if not (isinstance(value, int) and value <= 0):
        eng.wait_ge(sem, value)


def stand_alone(eng, s_passed):
    eng.sem_inc(s_passed, 1)


def build_tower(nc, ids, table, lora_b, w_slices, wo, gate, norm_w, rope, ident, mask, iota, out):
    ctx = ExitStack()
    with ctx:
        def sb(name, shape, dt=F32):
            return ctx.enter_context(nc.sbuf_tensor(name, shape, dt))

        def pb(name, shape, dt=F32):
            return ctx.enter_context(nc.psum_tensor(name, shape, dt))

        def sem(name):
            return ctx.enter_context(nc.semaphore(name))

        w_split = nc.dram_tensor("w_split", (NS, P, 2 * SL), F32, kind="Internal").ap()

        ident_f = sb("ident_f", [P, P])
        ident_b = sb("ident_b", [P, P], BF16)
        mask_b = sb("mask_b", [P, P], BF16)
        mask_f = sb("mask_f", [P, P])
        iota_e = sb("iota_e", [P, NE])
        half = sb("half", [P, 6])
        idx_all = sb("idx_all", [P, B * NT], I32)
        idx_cur = sb("idx_cur", [P, NT], I32)
        loraB = sb("loraB", [R, D])
        loraT = sb("loraT", [R, T])
        emb = sb("emb", [P, NT, D + R])
        h = sb("h", [P, 2, NT, D])
        norm_in = sb("norm_in", [P, 2, 2, HD // 2])
        cs = sb("cs", [P, 2, NT, HD // 2])
        tabA = sb("tabA", [P, NT, 3, HD])
        tabB = sb("tabB", [P, NT, 3, HD])
        W = sb("W", [P, 2, 2, KC, 512], F32R)
        wo_s = sb("wo_s", [P, 2, NH, D], F32R)
        gate_f = sb("gate_f", [P, KC * NE])
        gate_s = sb("gate_s", [P, 2, KC * NE], F32R)
        xn = sb("xn", [P, NT, D])
        lnT = [sb(f"ln{i}T", [P, 2, KC, T], F32R) for i in (1, 2)]
        stats = sb("stats", [P, NT, 6])
        mv = sb("mv", [P, NT, 2])
        std = sb("std", [P, NT])
        rstd = sb("rstd", [P, NT])
        sq_junk = sb("sq_junk", [P, 4, HD])
        ssq = sb("ssq", [P, NT, 3])
        rms = sb("rms", [P, NT, 3])
        rinv = sb("rinv", [P, NT, 3])
        ropeA = sb("ropeA", [P, NT, 3, HD])
        ropeB = sb("ropeB", [P, NT, 3, HD])
        vraw = sb("vraw", [P, NT, HD])
        V = sb("V", [P, 2, NT, HD], F32R)
        qkT = sb("qkT", [P, 2, 3, T], F32R)
        nbias = sb("nbias", [P, U])
        rowsum = sb("rowsum", [P, U])
        rsum = sb("rsum", [P, U])
        prob = sb("prob", [P, 4, T])
        pT = sb("pT", [P, REP, 2, NT, T], F32R)
        yT = sb("yT", [P, REP, 2, T], F32R)
        logits = sb("logits", [P, NT, NE])
        top8 = sb("top8", [P, NT, 8])
        top8i = sb("top8i", [P, NT, 8], U32)
        topf = sb("topf", [P, NT, 2])
        gdiff = sb("gdiff", [P, NT])
        gexp = sb("gexp", [P, NT])
        gden = sb("gden", [P, NT])
        gw = sb("gw", [P, 2, NT])
        hot = sb("hot", [P, 2, NT, NE])
        wfull = sb("wfull", [P, NT, NE])

        pj = [pb(f"pj{i}", [P, 512]) for i in range(2)]
        tp = [pb(f"tp{i}", [P, NT, P]) for i in range(2)]
        sc = [pb(f"sc{i}", [P, T]) for i in range(2)]
        ov = pb("ov", [P, T])
        op = pb("op", [P, 2, D])

        s_const = sem("s_const")
        s_gatehi = sem("s_gatehi")
        s_passed_dve = sem("s_passed_dve")
        s_passed_pool = sem("s_passed_pool")
        s_tab = sem("s_tab")
        s_stage = [sem(f"s_stage{i}") for i in range(2)]
        s_split_hi = sem("s_split_hi")
        s_split_lo = sem("s_split_lo")
        s_wstore = [sem(f"s_wstore{i}") for i in range(2)]
        s_wload = sem("s_wload")
        s_idx = sem("s_idx")
        s_gather = sem("s_gather")
        s_loraT = sem("s_loraT")
        s_loraC = sem("s_loraC")
        s_loraM = sem("s_loraM")
        s_emb = sem("s_emb")
        s_stat = sem("s_stat")
        s_aggr = sem("s_aggr")
        s_var = sem("s_var")
        s_std = sem("s_std")
        s_rstd = sem("s_rstd")
        s_xn = sem("s_xn")
        s_xt = sem("s_xt")
        s_xh = sem("s_xh")
        s_xl = sem("s_xl")
        s_pj = sem("s_pj")
        s_sq = sem("s_sq")
        s_vraw = sem("s_vraw")
        s_rope = sem("s_rope")
        s_radd = sem("s_radd")
        s_root = sem("s_root")
        s_rms = sem("s_rms")
        s_rinv = sem("s_rinv")
        s_qkn = sem("s_qkn")
        s_qkn_late = sem("s_qkn_late")
        s_qkT = sem("s_qkT")
        s_qkh = sem("s_qkh")
        s_qkl = sem("s_qkl")
        s_vh = sem("s_vh")
        s_vl = sem("s_vl")
        s_score = sem("s_score")
        s_bias = sem("s_bias")
        s_exp = sem("s_exp")
        s_rsum = sem("s_rsum")
        s_prob = sem("s_prob")
        s_pT = sem("s_pT")
        s_pTh = sem("s_pTh")
        s_pTl = sem("s_pTl")
        s_pv = sem("s_pv")
        s_yh = sem("s_yh")
        s_yl = sem("s_yl")
        s_op = sem("s_op")
        s_hadd = sem("s_hadd")
        s_gate = sem("s_gate")
        s_rt = sem("s_rt")
        s_rw = sem("s_rw")
        s_gdiff = sem("s_gdiff")
        s_gexp = sem("s_gexp")
        s_ff = sem("s_ff")
        s_ffc = sem("s_ffc")
        s_stored = sem("s_stored")

        TABS = 3 * NT + 2
        CONSTS = 8

        block = ctx.enter_context(nc.Block())

        def norm_events(b, last):
            return (None, 2 * b + 1) if last else (2 * b + 1, 2 * b + 2)

        WO_PIECES = 4
        SLICE_STEPS = NS - 2

        @block.sync
        def _(sp):
            for dst, src in ((ident_f[:], ident), (norm_in[:], norm_w), (cs[:], rope),
                             (iota_e[:], iota), (loraB[:], lora_b), (gate_f[:], gate), (mask_f[:], mask),
                             (idx_all[:], ids)):
                sp.dma_start(dst, src).then_inc(s_const, 16)

            for q in range(WO_PIECES):
                wait_past(sp, s_split_hi, q - 1)
                wait_past(sp, s_split_lo, q - 1)
                sp.dma_start(prob[:, 2 * (q % 2):2 * (q % 2) + 2, :].rearrange("p a n -> p (a n)"),
                             wo[:, q * SL:(q + 1) * SL]).then_inc(s_stage[q % 2], 16)

            def load_piece(i, s, k):
                sp.wait_ge(s_split_hi, WO_PIECES + i - 1)
                sp.wait_ge(s_split_lo, WO_PIECES + i - 1)
                sp.dma_start(prob[:, 2 * k:2 * k + 2, :].rearrange("p a n -> p (a n)"),
                             w_slices[bass.ds(s, 1), :, :].rearrange("a p n -> p (a n)"))\
                    .then_inc(s_stage[k], 16)

            with sp.Fori(0, SLICE_STEPS // 2) as j:
                for k in range(2):
                    load_piece(2 * j + k, 2 * j + k + 2, k)
            for k in range(2):
                load_piece(SLICE_STEPS + k, k, k)
            for k in range(2):
                sp.wait_ge(s_wstore[k], 16 * (NS // 2))

            def sequence(b, last):
                for j in range(NS):
                    if j == NKV - 1 and last:
                        continue
                    slot = (j + 1) % 2
                    before = NS * b + j - (1 if last and j >= NKV else 0)
                    if j == 0:
                        if not (isinstance(b, int) and b == 0):
                            sp.wait_ge(s_ff, 16 * b - NT)
                        s = 1
                    elif j == 1:
                        if isinstance(b, int) and b == 0:
                            sp.wait_ge(s_pj, NT)
                        else:
                            sp.wait_ge(s_ff, 16 * b)
                        s = 2
                    elif j <= NKV:
                        sp.wait_ge(s_pj, NT * (NKV * b + j))
                        s = (j + 1) % NKV if j < NKV else NKV
                    elif j == NKV + 1:
                        sp.wait_ge(s_pj, NT * (NKV * b + NKV + (0 if last else 1)))
                        s = j
                    else:
                        sp.wait_ge(s_ff, 16 * b + NT * (j - NKV - 1))
                        s = j
                    wait_past(sp, s_wload, 16 * before)
                    sp.dma_start(W[:, slot].rearrange("p a k n -> p (a k n)").bitcast(F32), w_split[s])\
                        .then_inc(s_wload, 16)
                sp.wait_ge(s_ffc, 2 * 16 * (b + 1))
                sp.dma_start(out[bass.ds(b, 1)].rearrange("a (t p) d -> p (a t) d", p=P),
                             h[:, bass.ds(b % 2, 1)].rearrange("p a t d -> p (a t) d"))\
                    .then_inc(s_stored, 16)

            sequence(0, False)
            with sp.Fori(1, B - 1) as b:
                sequence(b, False)
            sequence(B - 1, True)
            sp.wait_ge(s_stored, 16 * (B + 1))

        def wload_count(b, j, last):
            return 16 * (NS * b + j + 1 - (1 if last and j >= NKV else 0))

        @block.gpsimd
        def _(pool):
            nc.gpsimd.memset(half[:], 0.5).then_inc(s_stored, 16)

            def fetch(b):
                nc.gpsimd.tensor_copy(idx_cur[:], idx_all[:, bass.ds(b * NT, NT)]).then_inc(s_idx, 1)
                pool.wait_ge(s_idx, b + 1)
                stand_alone(pool, s_passed_pool)
                for t in range(NT):
                    nc.gpsimd.indirect_dma_start(
                        out=emb[:, t, :], out_offset=None, in_=table,
                        in_offset=bass.IndirectOffsetOnAxis(ap=idx_cur[:, t:t + 1], axis=0))\
                        .then_inc(s_gather, 16)

            def norm_root(e):
                pool.wait_ge(s_aggr, NT * (e + 1))
                stand_alone(pool, s_passed_pool)
                nc.gpsimd.tensor_scalar(std[:], mv[:, :, 1], LN_EPS, 1.0, ALU.add, ALU.mult)\
                    .then_inc(s_var, 1)
                pool.wait_ge(s_var, e + 1)
                nc.gpsimd.tensor_tensor(std[:], std[:], half[:, 0:NT], ALU.pow).then_inc(s_std, 1)

            def rotate_sum(n, t):
                pool.wait_ge(s_rope, NT * n + t + 1)
                nc.gpsimd.tensor_tensor(ropeA[:, t], ropeA[:, t], ropeB[:, t], ALU.add)\
                    .then_inc(s_radd, 1)

            def head_rms(n, pair):
                def rows(x):
                    return x[:, 2 * pair:2 * pair + 2].rearrange("p t c -> p (t c)")

                pool.wait_ge(s_sq, 12 * n + 6 * (pair + 1))
                nc.gpsimd.tensor_tensor(rows(rms), rows(ssq), half[:, 0:6], ALU.pow).then_inc(s_root, 1)
                pool.wait_ge(s_root, 2 * n + pair + 1)
                stand_alone(pool, s_passed_pool)
                nc.gpsimd.tensor_scalar(rows(rms), rows(rms), RMS_EPS, 1.0, ALU.add, ALU.mult)\
                    .then_inc(s_rms, 1)

            def norm_heads(n, t):
                if t == 0:
                    pool.wait_ge(s_rinv, 2 * n + 1)
                pool.wait_ge(s_radd, NT * n + t + 1)
                nc.gpsimd.tensor_tensor(ropeA[:, t], ropeA[:, t],
                                        rinv[:, t][:, :, None].to_broadcast([P, 3, HD]), ALU.mult)\
                    .then_inc(s_qkn, 1)

            def normalise(n, u):
                pool.wait_ge(s_rsum, U * n + u + 1)
                stand_alone(pool, s_passed_pool)
                w = (u % NT + 1) * P
                nc.gpsimd.tensor_scalar(prob[:, u % 4, 0:w], prob[:, u % 4, 0:w], rsum[:, u:u + 1],
                                        1.0, ALU.mult, ALU.mult).then_inc(s_prob, 1)

            def group(n):
                for u in range(U):
                    if u + 2 < U:
                        normalise(n, u + 2)
                    if u == 2:
                        head_rms(n + 1, 0)
                    if u == 3:
                        norm_heads(n + 1, 0)
                        norm_heads(n + 1, 1)
                    if u < NT:
                        rotate_sum(n + 1, u)
                    if u == 4:
                        head_rms(n + 1, 1)
                normalise(n + 1, 0)
                normalise(n + 1, 1)

            def sequence(b, last):
                n = NKV * b + NKV - 1
                if not last:
                    pool.wait_ge(s_emb, 2 * (b + 1))
                    fetch(b + 1)
                group(NKV * b)
                with pool.Fori(1, NKV - 1) as g:
                    group(NKV * b + g)
                e1, e2 = norm_events(b, last)
                for u in range(U):
                    if u + 2 < U:
                        normalise(n, u + 2)
                    if u == 1 and not last:
                        norm_root(e1)
                    if u >= 5 and not last:
                        rotate_sum(n + 1, u - 5)
                    if u == 7 and not last:
                        head_rms(n + 1, 0)
                if not last:
                    rotate_sum(n + 1, 3)
                    head_rms(n + 1, 1)
                    norm_heads(n + 1, 0)
                    norm_heads(n + 1, 1)
                norm_root(e2)
                if not last:
                    normalise(n + 1, 0)
                    normalise(n + 1, 1)

            pool.wait_ge(s_const, 16 * CONSTS)
            fetch(0)
            norm_root(0)
            for t in range(NT):
                rotate_sum(0, t)
            head_rms(0, 0)
            head_rms(0, 1)
            norm_heads(0, 0)
            norm_heads(0, 1)
            normalise(0, 0)
            normalise(0, 1)
            with pool.Fori(0, B - 1) as b:
                sequence(b, False)
            sequence(B - 1, True)

        @block.scalar
        def _(act):
            copy = ACT.Copy

            def split_piece(i, k, dst):
                nc.scalar.activation(dst, prob[:, 2 * k:2 * k + 2, :].rearrange("p a n -> p (a n)"),
                                     copy).then_inc(s_split_hi, 1)

            act.wait_ge(s_const, 16 * CONSTS)
            nc.scalar.activation(gate_s[:, 0], gate_f[:], copy).then_inc(s_gatehi, 1)
            for q in range(WO_PIECES):
                act.wait_ge(s_stage[q % 2], 16 * (q // 2 + 1))
                split_piece(q, q % 2, wo_s[:, 0, 4 * q:4 * q + 4, :].rearrange("p a n -> p (a n)"))

            def slice_piece(i, s, j, k):
                act.wait_ge(s_stage[k], 16 * (WO_PIECES // 2 + j + 1))
                if not (isinstance(i, int) and i < 2):
                    act.wait_ge(s_wstore[k], 16 * j)
                split_piece(i, k, W[:, k, 0].rearrange("p k n -> p (k n)"))
                act.wait_ge(s_split_hi, WO_PIECES + i + 1)
                act.wait_ge(s_split_lo, WO_PIECES + i + 1)
                act.dma_start(w_split[bass.ds(s, 1)].rearrange("a p n -> p (a n)"),
                              W[:, k].rearrange("p a k n -> p (a k n)").bitcast(F32)).then_inc(s_wstore[k], 16)

            for k in range(2):
                slice_piece(k, k + 2, 0, k)
            with act.Fori(1, SLICE_STEPS // 2) as j:
                for k in range(2):
                    slice_piece(2 * j + k, 2 * j + k + 2, j, k)
            for k in range(2):
                slice_piece(SLICE_STEPS + k, k, SLICE_STEPS // 2, k)

            def lora_copy(b):
                act.wait_ge(s_loraT, b + 1)
                nc.scalar.activation(loraT[:], pj[0][0:R, :], copy).then_inc(s_loraC, 1)

            def normed_hi(e, which):
                for t in range(NT):
                    act.wait_ge(s_xt, NT * e + t + 1)
                    nc.scalar.activation(lnT[which][:, 0, :, t * P:(t + 1) * P], tp[t % 2][:, 0:KC, :],
                                         copy).then_inc(s_xh, 1)

            def squares(n, t):
                act.wait_ge(s_pj, NT * n + t + 1)
                for c in range(3):
                    wait_past(act, s_sq, 12 * n + 3 * t + c - 3)
                    nc.scalar.activation(sq_junk[:, (3 * t + c) % 4], pj[t % 2][:, c * HD:(c + 1) * HD],
                                         ACT.Square, scale=float(HD) ** -0.5,
                                         accum_out=ssq[:, t, c:c + 1]).then_inc(s_sq, 1)
                if t == 0:
                    wait_past(act, s_vl, n)
                nc.scalar.activation(vraw[:, t], pj[t % 2][:, 3 * HD:], copy).then_inc(s_vraw, 1)

            def queries_hi(n, t):
                act.wait_ge(s_qkT, NT * n + t + 1)
                nc.scalar.activation(qkT[:, 0, :, t * P:(t + 1) * P], tp[t % 2][:, 0:3, :], copy)\
                    .then_inc(s_qkh, 1)

            def values_hi(n):
                act.wait_ge(s_vraw, NT * (n + 1))
                nc.scalar.activation(V[:, 0], vraw[:], copy).then_inc(s_vh, 1)

            def exponential(n, u):
                act.wait_ge(s_bias, U * n + u + 1)
                w = (u % NT + 1) * P
                nc.scalar.activation(prob[:, u % 4, 0:w], sc[u % 2][:, 0:w], ACT.Exp,
                                     bias=nbias[:, u:u + 1],
                                     accum_out=rowsum[:, u:u + 1]).then_inc(s_exp, 1)

            def probs_hi(n, u):
                act.wait_ge(s_pT, U * n + u + 1)
                t = u % NT
                nc.scalar.activation(pT[:, u // NT, 0, 0:t + 1, t * P:(t + 1) * P],
                                     tp[u % 2][:, 0:t + 1, :], copy).then_inc(s_pTh, 1)

            def heads_hi(n, r):
                act.wait_ge(s_pv, REP * n + r + 1)
                nc.scalar.activation(yT[:, r, 0], ov[:], copy).then_inc(s_yh, 1)

            def group(n, carry):
                for u in range(U):
                    if u < NT:
                        squares(n + 1, u)
                    if u == 6:
                        queries_hi(n + 1, 0)
                        queries_hi(n + 1, 1)
                        if carry:
                            act.wait_ge(s_op, 2 * n)
                        heads_hi(n, 0)
                    probs_hi(n, u)
                    if u + 2 < U:
                        exponential(n, u + 2)
                    if u == 6:
                        exponential(n + 1, 0)
                        exponential(n + 1, 1)
                queries_hi(n + 1, 2)
                queries_hi(n + 1, 3)
                heads_hi(n, 1)
                values_hi(n + 1)

            def sequence(b, last):
                n = NKV * b + NKV - 1
                group(NKV * b, False)
                with act.Fori(1, NKV - 1) as g:
                    group(NKV * b + g, True)
                e1, e2 = norm_events(b, last)
                for u in range(U):
                    if not last:
                        if u == 0:
                            lora_copy(b + 1)
                        if u == 4:
                            normed_hi(e1, 0)
                        if u >= 5:
                            squares(n + 1, u - 5)
                    if u == 6:
                        heads_hi(n, 0)
                    probs_hi(n, u)
                    if u + 2 < U:
                        exponential(n, u + 2)
                if not last:
                    squares(n + 1, 3)
                heads_hi(n, 1)
                if not last:
                    values_hi(n + 1)
                    for t in range(NT):
                        queries_hi(n + 1, t)
                normed_hi(e2, 1)
                if not last:
                    exponential(n + 1, 0)
                    exponential(n + 1, 1)
                act.wait_ge(s_gdiff, b + 1)
                nc.scalar.activation(gexp[:], gdiff[:], ACT.Exp).then_inc(s_gexp, 1)

            lora_copy(0)
            normed_hi(0, 0)
            for t in range(NT):
                squares(0, t)
            values_hi(0)
            for t in range(NT):
                queries_hi(0, t)
            exponential(0, 0)
            exponential(0, 1)
            with act.Fori(0, B - 1) as b:
                sequence(b, False)
            sequence(B - 1, True)

        @block.vector
        def _(dve):
            def raw(x):
                return x.bitcast(F32)

            dve.wait_ge(s_const, 16 * CONSTS)
            nc.vector.tensor_scalar(norm_in[:, 0], norm_in[:, 0], ATT_SCALE, None, ALU.mult)\
                .then_inc(s_tab, 1)
            dve.wait_ge(s_tab, 1)
            for c in range(3):
                wsel = norm_in[:, 0 if c < 2 else 1]
                for t in range(NT):
                    nc.vector.tensor_tensor(tabA[:, t, c].rearrange("p (a d) -> p a d", a=2), wsel,
                                            cs[:, 0, t][:, None, :].to_broadcast([P, 2, HD // 2]),
                                            ALU.mult)
                    nc.vector.tensor_tensor(tabB[:, t, c, HD // 2:], wsel[:, 0], cs[:, 1, t], ALU.mult)
                    nc.vector.scalar_tensor_tensor(tabB[:, t, c, 0:HD // 2], wsel[:, 1], -1.0,
                                                   cs[:, 1, t], ALU.mult, ALU.mult).then_inc(s_tab, 1)
            nc.vector.tensor_copy(ident_b[:], ident_f[:])
            nc.vector.tensor_copy(mask_b[:], mask_f[:]).then_inc(s_tab, 1)
            dve.wait_ge(s_tab, TABS)
            dve.wait_ge(s_gatehi, 1)
            nc.vector.tensor_tensor(gate_s[:, 1], gate_f[:], raw(gate_s[:, 0]), ALU.subtract)\
                .then_inc(s_tab, 1)

            def split_piece(i, k, hi, lo):
                dve.wait_ge(s_split_hi, i + 1)
                nc.vector.tensor_tensor(lo, prob[:, 2 * k:2 * k + 2, :].rearrange("p a n -> p (a n)"),
                                        raw(hi), ALU.subtract).then_inc(s_split_lo, 1)

            for q in range(WO_PIECES):
                hi, lo = (wo_s[:, x, 4 * q:4 * q + 4, :].rearrange("p a n -> p (a n)") for x in range(2))
                split_piece(q, q % 2, hi, lo)

            def slice_piece(i, k):
                hi, lo = (W[:, k, x].rearrange("p k n -> p (k n)") for x in range(2))
                split_piece(WO_PIECES + i, k, hi, lo)

            with dve.Fori(0, NS // 2) as j:
                for k in range(2):
                    slice_piece(2 * j + k, k)

            def embed(b):
                wait_past(dve, s_stored, 16 * b)
                for pair in range(2):
                    dve.wait_ge(s_loraM, 2 * b + pair + 1)
                    bank = pj[1 - pair][:].rearrange("p (t d) -> p t d", t=2)
                    nc.vector.scalar_tensor_tensor(
                        h[:, bass.ds(b % 2, 1), 2 * pair:2 * pair + 2].rearrange("p a t d -> p (a t) d"),
                        bank, LORA_SCALING, emb[:, 2 * pair:2 * pair + 2, 0:D], ALU.mult, ALU.add)\
                        .then_inc(s_emb, 1)

            def h_tile(b, t):
                return h[:, bass.ds(b % 2, 1), t].rearrange("p a d -> p (a d)")

            def norm_stats(e, b):
                stand_alone(dve, s_passed_dve)
                for t in range(NT):
                    nc.vector.bn_stats(stats[:, t], h_tile(b, t)).then_inc(s_stat, 1)
                for t in range(NT):
                    dve.wait_ge(s_stat, NT * e + t + 1)
                    stand_alone(dve, s_passed_dve)
                    nc.vector.bn_aggr(mv[:, t], stats[:, t]).then_inc(s_aggr, 1)

            def norm_apply(e, b):
                dve.wait_ge(s_std, e + 1)
                nc.vector.reciprocal(rstd[:], std[:]).then_inc(s_rstd, 1)
                dve.wait_ge(s_rstd, e + 1)
                for t in range(NT):
                    nc.vector.tensor_scalar(xn[:, t], h_tile(b, t), mv[:, t, 0:1], rstd[:, t:t + 1],
                                            ALU.subtract, ALU.mult).then_inc(s_xn, 1)

            def normed_lo(e, which):
                for t in range(NT):
                    dve.wait_ge(s_xh, NT * e + t + 1)
                    cols = slice(t * P, (t + 1) * P)
                    nc.vector.tensor_tensor(lnT[which][:, 1, :, cols], tp[t % 2][:, 0:KC, :],
                                            raw(lnT[which][:, 0, :, cols]), ALU.subtract)\
                        .then_inc(s_xl, 1)

            def rotate(n, t):
                dve.wait_ge(s_vraw, NT * n + t + 1)
                wait_past(dve, s_qkT, NT * (n - 1) + t + 1)
                qk = pj[t % 2][:, 0:3 * HD]
                nc.vector.tensor_tensor(ropeA[:, t], qk.rearrange("p (c d) -> p c d", c=3), tabA[:, t],
                                        ALU.mult)
                nc.vector.tensor_tensor(
                    ropeB[:, t].rearrange("p c (a d) -> p c a d", a=2),
                    qk.rearrange("p (c a d) -> p c a d", c=3, a=2)[:, :, ::-1, :],
                    tabB[:, t].rearrange("p c (a d) -> p c a d", a=2), ALU.mult).then_inc(s_rope, 1)

            def norm_factors(n, pair):
                dve.wait_ge(s_rms, 2 * n + pair + 1)
                nc.vector.reciprocal(rinv[:, 2 * pair:2 * pair + 2], rms[:, 2 * pair:2 * pair + 2])\
                    .then_inc(s_rinv, 1)

            def norm_heads(n, t):
                if t == 2:
                    dve.wait_ge(s_rinv, 2 * n + 2)
                dve.wait_ge(s_radd, NT * n + t + 1)
                nc.vector.tensor_tensor(ropeA[:, t], ropeA[:, t],
                                        rinv[:, t][:, :, None].to_broadcast([P, 3, HD]), ALU.mult)\
                    .then_inc(s_qkn_late, 1)

            def queries_lo(n, t):
                dve.wait_ge(s_qkh, NT * n + t + 1)
                cols = slice(t * P, (t + 1) * P)
                nc.vector.tensor_tensor(qkT[:, 1, :, cols], tp[t % 2][:, 0:3, :],
                                        raw(qkT[:, 0, :, cols]), ALU.subtract).then_inc(s_qkl, 1)

            def values_lo(n):
                dve.wait_ge(s_vh, n + 1)
                nc.vector.tensor_tensor(V[:, 1], vraw[:], raw(V[:, 0]), ALU.subtract).then_inc(s_vl, 1)

            def maximum(n, u):
                dve.wait_ge(s_score, U * n + u + 1)
                nc.vector.tensor_reduce(nbias[:, u:u + 1], sc[u % 2][:, 0:(u % NT + 1) * P], AX,
                                        ALU.max, negate=True).then_inc(s_bias, 1)

            def inverse_sum(n, u):
                dve.wait_ge(s_exp, U * n + u + 1)
                nc.vector.reciprocal(rsum[:, u:u + 1], rowsum[:, u:u + 1]).then_inc(s_rsum, 1)

            def probs_lo(n, u):
                dve.wait_ge(s_pTh, U * n + u + 1)
                r, t = u // NT, u % NT
                cols = slice(t * P, (t + 1) * P)
                nc.vector.tensor_tensor(pT[:, r, 1, 0:t + 1, cols], tp[u % 2][:, 0:t + 1, :],
                                        raw(pT[:, r, 0, 0:t + 1, cols]), ALU.subtract)\
                    .then_inc(s_pTl, 1)

            def heads_lo(n, r):
                dve.wait_ge(s_yh, REP * n + r + 1)
                nc.vector.tensor_tensor(yT[:, r, 1], ov[:], raw(yT[:, r, 0]), ALU.subtract)\
                    .then_inc(s_yl, 1)

            def add_attention(n, b, pair):
                dve.wait_ge(s_op, 2 * n + pair + 1)
                dst = h[:, bass.ds(b % 2, 1), 2 * pair:2 * pair + 2].rearrange("p a t d -> p (a t) d")
                nc.vector.tensor_tensor(dst, op[:], dst, ALU.add).then_inc(s_hadd, 1)

            def router(b):
                k = [6 * b]

                def step(ins):
                    k[0] = k[0] + 1
                    ins.then_inc(s_rt, 1)
                    dve.wait_ge(s_rt, k[0])

                dve.wait_ge(s_gate, b + 1)
                step(nc.vector.tensor_copy(logits[:].rearrange("p t e -> p (t e)"), ov[:, 0:NT * NE]))
                stand_alone(dve, s_passed_dve)
                for t in range(NT):
                    last = nc.vector.max(top8[:, t], logits[:, t])
                step(last)
                nc.vector.tensor_tensor(gdiff[:], top8[:, :, 1], top8[:, :, 0], ALU.subtract)\
                    .then_inc(s_gdiff, 1)
                stand_alone(dve, s_passed_dve)
                for t in range(NT):
                    last = nc.vector.max_index(top8i[:, t], top8[:, t], logits[:, t])
                step(last)
                step(nc.vector.tensor_copy(topf[:], top8i[:, :, 0:2]))
                for i in range(2):
                    nc.vector.tensor_tensor(hot[:, i], iota_e[:][:, None, :].to_broadcast([P, NT, NE]),
                                            topf[:, :, i:i + 1].to_broadcast([P, NT, NE]), ALU.is_equal)
                dve.wait_ge(s_gexp, b + 1)
                step(nc.vector.tensor_scalar(gden[:], gexp[:], 1.0, None, ALU.add))
                step(nc.vector.reciprocal(gw[:, 0], gden[:]))

            def router_weights(b):
                k = 3 * b
                nc.vector.tensor_tensor(gw[:, 1], gw[:, 0], gexp[:], ALU.mult).then_inc(s_rw, 1)
                dve.wait_ge(s_rw, k + 1)
                for i in range(2):
                    last = nc.vector.tensor_tensor(hot[:, i], hot[:, i],
                                                   gw[:, i][:, :, None].to_broadcast([P, NT, NE]), ALU.mult)
                last.then_inc(s_rw, 1)
                dve.wait_ge(s_rw, k + 2)
                nc.vector.tensor_tensor(wfull[:], hot[:, 0], hot[:, 1], ALU.add).then_inc(s_rw, 1)
                dve.wait_ge(s_rw, k + 3)

            def experts(b):
                for f in range(NCH * NT):
                    c, t = divmod(f, NT)
                    dve.wait_ge(s_ff, 16 * b + f + 1)
                    for i in range(EPC):
                        if i:
                            dve.wait_ge(s_ffc, 32 * b + 2 * f + 1)
                        e = EPC * c + i
                        nc.vector.scalar_tensor_tensor(h_tile(b, t), pj[f % 2][:, i * D:(i + 1) * D],
                                                       wfull[:, t, e:e + 1], h_tile(b, t),
                                                       ALU.mult, ALU.add).then_inc(s_ffc, 1)

            def group(n, b, carry):
                for u in range(U):
                    if carry and u == 5:
                        add_attention(n - 1, b, 0)
                    if u + 2 < U:
                        maximum(n, u + 2)
                    if u < NT:
                        rotate(n + 1, u)
                    if u == 6:
                        queries_lo(n + 1, 0)
                        queries_lo(n + 1, 1)
                        if carry:
                            add_attention(n - 1, b, 1)
                        heads_lo(n, 0)
                    probs_lo(n, u)
                    if u + 2 < U:
                        inverse_sum(n, u + 2)
                    if u == 3:
                        norm_factors(n + 1, 0)
                    if u == 6:
                        norm_factors(n + 1, 1)
                        maximum(n + 1, 0)
                        norm_heads(n + 1, 2)
                        maximum(n + 1, 1)
                        norm_heads(n + 1, 3)
                inverse_sum(n + 1, 0)
                inverse_sum(n + 1, 1)
                queries_lo(n + 1, 2)
                queries_lo(n + 1, 3)
                heads_lo(n, 1)
                values_lo(n + 1)

            def sequence(b, last):
                n = NKV * b + NKV - 1
                group(NKV * b, b, False)
                with dve.Fori(1, NKV - 1) as g:
                    group(NKV * b + g, b, True)
                e1, e2 = norm_events(b, last)
                for u in range(U):
                    if u == 1 and not last:
                        embed(b + 1)
                    if u == 4 and not last:
                        normed_lo(e1, 0)
                    if u + 2 < U:
                        maximum(n, u + 2)
                    if u == 1 and not last:
                        dve.wait_ge(s_emb, 2 * (b + 2))
                        norm_stats(e1, b + 1)
                    if u >= 5 and not last:
                        rotate(n + 1, u - 5)
                    if u == 6:
                        heads_lo(n, 0)
                    probs_lo(n, u)
                    if u in (2, 3):
                        add_attention(n - 1, b, u - 2)
                    if u + 2 < U:
                        inverse_sum(n, u + 2)
                    if u == 2 and not last:
                        norm_apply(e1, b + 1)
                if not last:
                    rotate(n + 1, 3)
                    for pair in range(2):
                        norm_factors(n + 1, pair)
                    for t in range(2, NT):
                        norm_heads(n + 1, t)
                heads_lo(n, 1)
                if not last:
                    values_lo(n + 1)
                for pair in range(2):
                    add_attention(n, b, pair)
                dve.wait_ge(s_hadd, 1 + 2 * (n + 1))
                norm_stats(e2, b)
                if not last:
                    queries_lo(n + 1, 0)
                    queries_lo(n + 1, 1)
                norm_apply(e2, b)
                if not last:
                    queries_lo(n + 1, 2)
                    queries_lo(n + 1, 3)
                normed_lo(e2, 1)
                if not last:
                    maximum(n + 1, 0)
                    maximum(n + 1, 1)
                    inverse_sum(n + 1, 0)
                    inverse_sum(n + 1, 1)
                router(b)
                router_weights(b)
                experts(b)

            dve.sem_inc(s_hadd, 1)
            embed(0)
            dve.wait_ge(s_emb, 2)
            norm_stats(0, 0)
            norm_apply(0, 0)
            normed_lo(0, 0)
            for t in range(NT):
                rotate(0, t)
            for pair in range(2):
                norm_factors(0, pair)
            for t in range(2, NT):
                norm_heads(0, t)
            values_lo(0)
            for t in range(NT):
                queries_lo(0, t)
            maximum(0, 0)
            maximum(0, 1)
            inverse_sum(0, 0)
            inverse_sum(0, 1)
            with dve.Fori(0, B - 1) as b:
                sequence(b, False)
            sequence(B - 1, True)

        @block.tensor
        def _(pe):
            mm = nc.tensor.matmul

            def three_pass(dst, lhs, rhs, start, stop):
                mm(dst, lhs[0], rhs[0], start=start, stop=False)
                mm(dst, lhs[0], rhs[1], start=False, stop=False)
                return mm(dst, lhs[1], rhs[0], start=False, stop=stop)

            def lora_transpose(b, n):
                pe.wait_ge(s_gather, 64 * (b + 1))
                wait_past(pe, s_rope, NT * n + 3)
                wait_past(pe, s_vraw, NT * n + 3)
                for t in range(NT):
                    last = nc.tensor.transpose(pj[0][0:R, t * P:(t + 1) * P], emb[:, t, D:D + R],
                                               ident_f[:])
                last.then_inc(s_loraT, 1)

            def lora_product(b, n):
                pe.wait_ge(s_loraC, b + 1)
                wait_past(pe, s_rope, NT * n + 4)
                wait_past(pe, s_vraw, NT * n + 4)
                for pair in range(2):
                    for i in range(2):
                        t = 2 * pair + i
                        last = mm(pj[1 - pair][:, i * D:(i + 1) * D], loraT[:, t * P:(t + 1) * P],
                                  loraB[:], start=True, stop=True)
                    last.then_inc(s_loraM, 1)

            def norm_transpose(e, before):
                for t in range(NT):
                    pe.wait_ge(s_xn, NT * e + t + 1)
                    if t < 2:
                        wait_past(pe, *before[t])
                    else:
                        pe.wait_ge(s_xl, NT * e + t - 1)
                    for k in range(KC):
                        last = nc.tensor.transpose(tp[t % 2][:, k], xn[:, t, k * P:(k + 1) * P], ident_f[:])
                    last.then_inc(s_xt, 1)

            def project(n, t, slot, bank_free):
                for s, v in bank_free:
                    wait_past(pe, s, v)
                for k in range(KC):
                    last = three_pass(pj[t % 2][:], [lnT[0][:, x, k, t * P:(t + 1) * P] for x in range(2)],
                                      [W[:, bass.ds(slot, 1), x, k, :].rearrange("p a n -> p (a n)")
                                       for x in range(2)], start=k == 0, stop=k == KC - 1)
                last.then_inc(s_pj, 1)

            def bank_read(n, t):
                return [(s_rope, NT * n + t + 1), (s_vraw, NT * n + t + 1)]

            def qk_transpose(n, t, before):
                if t < 2:
                    pe.wait_ge(s_qkn, 2 * n + t + 1)
                else:
                    pe.wait_ge(s_qkn_late, 2 * n + t - 1)
                wait_past(pe, *before)
                for c in range(3):
                    last = nc.tensor.transpose(tp[t % 2][:, c], ropeA[:, t, c], ident_f[:])
                last.then_inc(s_qkT, 1)

            def score(n, u):
                r, t = u // NT, u % NT
                pe.wait_ge(s_qkl, NT * n + t + 1)
                w = (t + 1) * P
                if u >= 2:
                    pe.wait_ge(s_exp, U * n + u - 1)
                else:
                    wait_past(pe, s_exp, U * (n - 1) + u + 7)
                three_pass(sc[u % 2][:, 0:w], [qkT[:, x, r, t * P:(t + 1) * P] for x in range(2)],
                           [qkT[:, x, 2, 0:w] for x in range(2)], start=True, stop=False)
                mm(sc[u % 2][:, t * P:w], ident_b[:], mask_b[:], start=False, stop=True)\
                    .then_inc(s_score, 1)

            def prob_transpose(n, u, before):
                pe.wait_ge(s_prob, U * n + u + 1)
                wait_past(pe, *before)
                for kt in range(u % NT + 1):
                    last = nc.tensor.transpose(tp[u % 2][:, kt], prob[:, u % 4, kt * P:(kt + 1) * P],
                                               ident_f[:])
                last.then_inc(s_pT, 1)

            def value_product(n, r):
                pe.wait_ge(s_pTl, U * n + NT * (r + 1))
                if r == 0:
                    pe.wait_ge(s_vl, n + 1)
                else:
                    pe.wait_ge(s_yl, REP * n + r)
                for kt in range(NT):
                    last = three_pass(ov[:, kt * P:], [V[:, x, kt] for x in range(2)],
                                      [pT[:, r, x, kt, kt * P:] for x in range(2)],
                                      start=kt == 0, stop=kt == NT - 1)
                last.then_inc(s_pv, 1)

            def output_product(n, g, pair):
                pe.wait_ge(s_yl, REP * (n + 1))
                pe.wait_ge(s_hadd, 2 * n + 1 + pair)
                for i in range(2):
                    t = 2 * pair + i
                    for r in range(REP):
                        last = three_pass(
                            op[:, i], [yT[:, r, x, t * P:(t + 1) * P] for x in range(2)],
                            [wo_s[:, x, bass.ds(REP * g + r, 1), :].rearrange("p a d -> p (a d)")
                             for x in range(2)], start=r == 0, stop=r == REP - 1)
                last.then_inc(s_op, 1)

            def before_probs(n, u):
                if u < 2:
                    return s_qkl, NT * n + u + 3
                if u < 6:
                    return s_pTl, U * n + u - 1
                return s_qkl, NT * (n + 1) + u - 5

            def before_qk(n, t):
                return s_pTl, U * (n - 1) + t + 5

            def group(n, b, g, carry):
                for u in range(U):
                    if u < NT:
                        if u == 0:
                            pe.wait_ge(s_wload, 16 * (NS * b + g + 1))
                        project(n + 1, u, (g + 1) % 2,
                                bank_read(n, u + 2) if u < 2 else bank_read(n + 1, u - 2))
                    if carry and u == 4:
                        output_product(n - 1, g - 1, 0)
                    if u == 5:
                        value_product(n, 0)
                    if u == 6:
                        qk_transpose(n + 1, 0, before_qk(n + 1, 0))
                        qk_transpose(n + 1, 1, before_qk(n + 1, 1))
                        if carry:
                            output_product(n - 1, g - 1, 1)
                    prob_transpose(n, u, before_probs(n, u))
                    if u + 2 < U:
                        score(n, u + 2)
                    if u == 6:
                        score(n + 1, 0)
                        score(n + 1, 1)
                qk_transpose(n + 1, 2, before_qk(n + 1, 2))
                qk_transpose(n + 1, 3, before_qk(n + 1, 3))
                value_product(n, 1)

            def sequence(b, last):
                n = NKV * b + NKV - 1
                group(NKV * b, b, 0, False)
                with pe.Fori(1, NKV - 1) as g:
                    group(NKV * b + g, b, g, True)
                e1, e2 = norm_events(b, last)
                for u in range(U):
                    if not last:
                        if u == 0:
                            lora_transpose(b + 1, n)
                        if u == 1:
                            lora_product(b + 1, n)
                        if u == 4:
                            norm_transpose(e1, [(s_pTl, U * n + 3), (s_pTl, U * n + 4)])
                        if u == 5:
                            pe.wait_ge(s_wload, wload_count(b, NKV - 1, last))
                            project(n + 1, 0, 0, [(s_emb, 2 * (b + 2)), (s_xl, NT * e1 + NT)])
                        if u == 6:
                            project(n + 1, 1, 0, [])
                        if u == 7:
                            project(n + 1, 2, 0, bank_read(n + 1, 0))
                    if u in (2, 3):
                        output_product(n - 1, NKV - 2, u - 2)
                    if u == 6:
                        value_product(n, 0)
                    if u < 2:
                        before = s_qkl, NT * n + u + 3
                    elif u in (4, 5) and not last:
                        before = s_xl, NT * e1 + u - 1
                    else:
                        before = s_pTl, U * n + u - 1
                    prob_transpose(n, u, before)
                    if u + 2 < U:
                        score(n, u + 2)
                if not last:
                    project(n + 1, 3, 0, bank_read(n + 1, 1))
                value_product(n, 1)
                for pair in range(2):
                    output_product(n, NKV - 1, pair)
                if not last:
                    for t in range(NT):
                        qk_transpose(n + 1, t, (s_pTl, U * n + 7 + t) if t < 2
                                     else (s_qkl, NT * (n + 1) + t - 1))
                    norm_transpose(e2, [(s_qkl, NT * (n + 1) + 3), (s_qkl, NT * (n + 1) + 4)])
                else:
                    norm_transpose(e2, [(s_pTl, U * n + 7), (s_pTl, U * n + 8)])
                if not last:
                    score(n + 1, 0)
                    score(n + 1, 1)
                pe.wait_ge(s_xl, NT * (e2 + 1))
                for t in range(NT):
                    for k in range(KC):
                        last_mm = three_pass(ov[:, t * NE:(t + 1) * NE],
                                             [lnT[1][:, x, k, t * P:(t + 1) * P] for x in range(2)],
                                             [gate_s[:, x, k * NE:(k + 1) * NE] for x in range(2)],
                                             start=k == 0, stop=k == KC - 1)
                last_mm.then_inc(s_gate, 1)
                for f in range(NCH * NT):
                    c, t = divmod(f, NT)
                    if t == 0:
                        pe.wait_ge(s_wload, wload_count(b, NKV + c, last))
                    if f < 2:
                        for s, v in bank_read(n if last else n + 1, f + 2):
                            pe.wait_ge(s, v)
                    else:
                        pe.wait_ge(s_ffc, 32 * b + 2 * (f - 1))
                    for k in range(KC):
                        last_mm = three_pass(pj[f % 2][:],
                                             [lnT[1][:, x, k, t * P:(t + 1) * P] for x in range(2)],
                                             [W[:, (NKV + c + 1) % 2, x, k, :] for x in range(2)],
                                             start=k == 0, stop=k == KC - 1)
                    last_mm.then_inc(s_ff, 1)
                if not last:
                    pe.wait_ge(s_ffc, 32 * (b + 1))

            pe.wait_ge(s_const, 16 * CONSTS)
            pe.wait_ge(s_tab, TABS + 1)
            lora_transpose(0, -1)
            lora_product(0, -1)
            norm_transpose(0, [(s_xn, 0), (s_xn, 0)])
            pe.wait_ge(s_split_lo, WO_PIECES + NS)
            for t in range(NT):
                pe.wait_ge(s_xl, t + 1)
                project(0, t, 0, [(s_emb, 2)] if t < 2 else bank_read(0, t - 2))
            for t in range(NT):
                qk_transpose(0, t, (s_xl, 3 + t) if t < 2 else (s_qkl, t - 1))
            score(0, 0)
            score(0, 1)
            with pe.Fori(0, B - 1) as b:
                sequence(b, False)
            sequence(B - 1, True)


def kernel(**inputs):
    import numpy as np
    import concourse.bacc as bacc
    from concourse.bass_utils import run_bass_kernel_spmd

    def arr(name):
        return np.asarray(inputs[name])

    table = np.concatenate([arr("L0_tok_emb_weight"), arr("L0_tok_lora_A").T], axis=1)
    ids = np.ascontiguousarray(arr("x").reshape(B * NT, P).T)
    def halves(w):
        return w.reshape(w.shape[0], -1, HD // 2, 2).transpose(0, 1, 3, 2).reshape(w.shape[0], -1, HD)

    wq = halves(arr("L0_attn_wq")).reshape(D, NKV, REP * HD)
    wk = halves(arr("L0_attn_wk"))
    wv = arr("L0_attn_wv").reshape(D, NKV, HD)
    qkv = np.concatenate([wq, wk, wv], axis=2).transpose(1, 0, 2)
    ew = arr("L0_ffn_expert_w").reshape(NCH, EPC * D, D).transpose(0, 2, 1)
    w_slices = np.concatenate([qkv, ew]).reshape(NS, KC, P, 512).transpose(0, 2, 1, 3)
    wo = arr("L0_attn_wo").reshape(NH, HD, D).transpose(1, 0, 2).reshape(HD, NH * D)
    gate = arr("L0_ffn_gate_w").T.reshape(KC, P, NE).transpose(1, 0, 2).reshape(P, KC * NE)
    norms = np.stack([arr("L0_attn_q_norm_w"), arr("L0_attn_k_norm_w")]).reshape(2, HD // 2, 2)
    norms = np.broadcast_to(norms.transpose(0, 2, 1), (P, 2, 2, HD // 2))
    theta = np.float32(1e6) ** (np.float32(-2.0) * np.arange(HD // 2, dtype=np.float32) / np.float32(HD))
    angle = np.arange(T, dtype=np.float32)[:, None] * theta[None, :].astype(np.float32)
    rope = np.stack([np.cos(angle), np.sin(angle)]).astype(np.float32)
    rope = rope.reshape(2, NT, P, HD // 2).transpose(2, 0, 1, 3)
    mask = np.triu(np.full((P, P), -3e37, np.float32), k=1)
    data = {
        "ids": ids, "table": table, "lora_b": arr("L0_tok_lora_B").T,
        "w_slices": w_slices.reshape(NS, P, SL), "wo": wo, "gate": gate, "norm_w": norms, "rope": rope,
        "ident": np.eye(P, dtype=np.float32), "mask": mask,
        "iota": np.broadcast_to(np.arange(NE, dtype=np.float32), (P, NE)),
    }
    nc = bacc.Bacc("TRN2", target_bir_lowering=False, num_devices=1)
    arrays, args = {}, {}
    for name, a in data.items():
        a = np.ascontiguousarray(a)
        arrays[f"in_{name}"] = a
        args[name] = nc.dram_tensor(f"in_{name}", a.shape, mybir.dt.from_np(a.dtype),
                                    kind="ExternalInput").ap()
    args["out"] = nc.dram_tensor("out_h", (B, T, D), F32, kind="ExternalOutput").ap()
    build_tower(nc, **args)
    r = run_bass_kernel_spmd(nc, [arrays], core_ids=[0])
    return r.results[0]["out_h"]
```

```python
from contextlib import ExitStack

import concourse.bass as bass
from concourse import mybir

F32 = mybir.dt.float32
F32R = mybir.dt.float32r
BF16 = mybir.dt.bfloat16
I32 = mybir.dt.int32
U32 = mybir.dt.uint32
ALU = mybir.AluOpType
ACT = mybir.ActivationFunctionType
AX = mybir.AxisListType.X

B, T, D = 8, 512, 256
R = 16
LORA_SCALING = 2.0
HD, NH, NKV = 128, 16, 8
REP = NH // NKV
NE = 8
P = 128
NT = T // P
KC = D // P
U = REP * NT
EPC = 2
NCH = NE // EPC
NS = NKV + NCH
SL = KC * 512
ATT_SCALE = float(HD) ** -0.5
RMS_EPS = 1e-6
LN_EPS = 1e-5


def wait_past(eng, sem, value):
    if not (isinstance(value, int) and value <= 0):
        eng.wait_ge(sem, value)


def stand_alone(eng, s_passed):
    eng.sem_inc(s_passed, 1)


def build_tower(nc, ids, table, lora_b, w_slices, wo, gate, norm_w, rope, ident, mask, iota, out):
    ctx = ExitStack()
    with ctx:
        def sb(name, shape, dt=F32):
            return ctx.enter_context(nc.sbuf_tensor(name, shape, dt))

        def pb(name, shape, dt=F32):
            return ctx.enter_context(nc.psum_tensor(name, shape, dt))

        def sem(name):
            return ctx.enter_context(nc.semaphore(name))

        w_split = nc.dram_tensor("w_split", (NS, P, 2 * SL), F32, kind="Internal").ap()

        ident_f = sb("ident_f", [P, P])
        ident_b = sb("ident_b", [P, P], BF16)
        mask_b = sb("mask_b", [P, P], BF16)
        mask_f = sb("mask_f", [P, P])
        iota_e = sb("iota_e", [P, NE])
        half = sb("half", [P, 6])
        idx_all = sb("idx_all", [P, B * NT], I32)
        idx_cur = sb("idx_cur", [P, NT], I32)
        loraB = sb("loraB", [R, D])
        loraT = sb("loraT", [R, T])
        emb = sb("emb", [P, NT, D + R])
        h = sb("h", [P, 2, NT, D])
        norm_in = sb("norm_in", [P, 2, 2, HD // 2])
        cs = sb("cs", [P, 2, NT, HD // 2])
        tabA = sb("tabA", [P, NT, 3, HD])
        tabB = sb("tabB", [P, NT, 3, HD])
        W = sb("W", [P, 2, 2, KC, 512], F32R)
        wo_s = sb("wo_s", [P, 2, NH, D], F32R)
        gate_f = sb("gate_f", [P, KC * NE])
        gate_s = sb("gate_s", [P, 2, KC * NE], F32R)
        xn = sb("xn", [P, NT, D])
        lnT = [sb(f"ln{i}T", [P, 2, KC, T], F32R) for i in (1, 2)]
        stats = sb("stats", [P, NT, 6])
        mv = sb("mv", [P, NT, 2])
        std = sb("std", [P, NT])
        rstd = sb("rstd", [P, NT])
        sq_junk = sb("sq_junk", [P, 4, HD])
        ssq = sb("ssq", [P, NT, 3])
        rms = sb("rms", [P, NT, 3])
        rinv = sb("rinv", [P, NT, 3])
        ropeA = sb("ropeA", [P, NT, 3, HD])
        ropeB = sb("ropeB", [P, NT, 3, HD])
        vraw = sb("vraw", [P, NT, HD])
        V = sb("V", [P, 2, NT, HD], F32R)
        qkT = sb("qkT", [P, 2, 3, T], F32R)
        nbias = sb("nbias", [P, U])
        rowsum = sb("rowsum", [P, U])
        rsum = sb("rsum", [P, U])
        prob = sb("prob", [P, 4, T])
        pT = sb("pT", [P, REP, 2, NT, T], F32R)
        yT = sb("yT", [P, REP, 2, T], F32R)
        logits = sb("logits", [P, NT, NE])
        top8 = sb("top8", [P, NT, 8])
        top8i = sb("top8i", [P, NT, 8], U32)
        topf = sb("topf", [P, NT, 2])
        gdiff = sb("gdiff", [P, NT])
        gexp = sb("gexp", [P, NT])
        gden = sb("gden", [P, NT])
        gw = sb("gw", [P, 2, NT])
        hot = sb("hot", [P, 2, NT, NE])
        wfull = sb("wfull", [P, NT, NE])

        pj = [pb(f"pj{i}", [P, 512]) for i in range(2)]
        tp = [pb(f"tp{i}", [P, NT, P]) for i in range(2)]
        sc = [pb(f"sc{i}", [P, T]) for i in range(2)]
        ov = pb("ov", [P, T])
        op = pb("op", [P, 2, D])

        s_const = sem("s_const")
        s_gatehi = sem("s_gatehi")
        s_passed_dve = sem("s_passed_dve")
        s_passed_pool = sem("s_passed_pool")
        s_tab = sem("s_tab")
        s_stage = [sem(f"s_stage{i}") for i in range(2)]
        s_split_hi = sem("s_split_hi")
        s_split_lo = sem("s_split_lo")
        s_wstore = [sem(f"s_wstore{i}") for i in range(2)]
        s_wload = sem("s_wload")
        s_idx = sem("s_idx")
        s_gather = sem("s_gather")
        s_loraT = sem("s_loraT")
        s_loraC = sem("s_loraC")
        s_loraM = sem("s_loraM")
        s_emb = sem("s_emb")
        s_stat = sem("s_stat")
        s_aggr = sem("s_aggr")
        s_var = sem("s_var")
        s_std = sem("s_std")
        s_rstd = sem("s_rstd")
        s_xn = sem("s_xn")
        s_xt = sem("s_xt")
        s_xh = sem("s_xh")
        s_xl = sem("s_xl")
        s_pj = sem("s_pj")
        s_sq = sem("s_sq")
        s_vraw = sem("s_vraw")
        s_rope = sem("s_rope")
        s_radd = sem("s_radd")
        s_root = sem("s_root")
        s_rms = sem("s_rms")
        s_rinv = sem("s_rinv")
        s_qkn = sem("s_qkn")
        s_qkT = sem("s_qkT")
        s_qkh = sem("s_qkh")
        s_qkl = sem("s_qkl")
        s_vh = sem("s_vh")
        s_vl = sem("s_vl")
        s_score = sem("s_score")
        s_bias = sem("s_bias")
        s_exp = sem("s_exp")
        s_rsum = sem("s_rsum")
        s_prob = sem("s_prob")
        s_prob_late = sem("s_prob_late")
        s_pT = sem("s_pT")
        s_pTh = sem("s_pTh")
        s_pTl = sem("s_pTl")
        s_pv = sem("s_pv")
        s_yh = sem("s_yh")
        s_yl = sem("s_yl")
        s_op = sem("s_op")
        s_hadd = sem("s_hadd")
        s_gate = sem("s_gate")
        s_rt = sem("s_rt")
        s_rw = sem("s_rw")
        s_gdiff = sem("s_gdiff")
        s_gexp = sem("s_gexp")
        s_ff = sem("s_ff")
        s_ffc = sem("s_ffc")
        s_stored = sem("s_stored")

        TABS = 3 * NT + 2
        CONSTS = 8

        block = ctx.enter_context(nc.Block())

        WO_PIECES = 4
        SLICE_STEPS = NS - 2

        @block.sync
        def _(sp):
            for dst, src in ((ident_f[:], ident), (norm_in[:], norm_w), (cs[:], rope),
                             (iota_e[:], iota), (loraB[:], lora_b), (gate_f[:], gate), (mask_f[:], mask),
                             (idx_all[:], ids)):
                sp.dma_start(dst, src).then_inc(s_const, 16)

            for q in range(WO_PIECES):
                wait_past(sp, s_split_hi, q - 1)
                wait_past(sp, s_split_lo, q - 1)
                sp.dma_start(prob[:, 2 * (q % 2):2 * (q % 2) + 2, :].rearrange("p a n -> p (a n)"),
                             wo[:, q * SL:(q + 1) * SL]).then_inc(s_stage[q % 2], 16)

            def load_piece(i, s, k):
                sp.wait_ge(s_split_hi, WO_PIECES + i - 1)
                sp.wait_ge(s_split_lo, WO_PIECES + i - 1)
                sp.dma_start(prob[:, 2 * k:2 * k + 2, :].rearrange("p a n -> p (a n)"),
                             w_slices[bass.ds(s, 1), :, :].rearrange("a p n -> p (a n)"))\
                    .then_inc(s_stage[k], 16)

            with sp.Fori(0, SLICE_STEPS // 2) as j:
                for k in range(2):
                    load_piece(2 * j + k, 2 * j + k + 2, k)
            for k in range(2):
                load_piece(SLICE_STEPS + k, k, k)
            for k in range(2):
                sp.wait_ge(s_wstore[k], 16 * (NS // 2))

            def load(s, before):
                wait_past(sp, s_wload, 16 * before)
                sp.dma_start(W[:, s % 2].rearrange("p a k n -> p (a k n)").bitcast(F32), w_split[s])\
                    .then_inc(s_wload, 16)

            def store(b):
                sp.wait_ge(s_ffc, 2 * 16 * (b + 1))
                sp.dma_start(out[bass.ds(b, 1)].rearrange("a (t p) d -> p (a t) d", p=P),
                             h[:, bass.ds(b % 2, 1)].rearrange("p a t d -> p (a t) d"))\
                    .then_inc(s_stored, 16)

            def sequence(b, first, last):
                done = NS * b
                for s in range(2, NKV):
                    if s > 3 or first:
                        sp.wait_ge(s_pj, NT * (NKV * b + s - 1))
                    else:
                        sp.wait_ge(s_ff, 16 * b - NT * (3 - s))
                    load(s, done)
                    done = done + 1
                    if s == 3 and not first:
                        store(b - 1)
                if not last:
                    for s in range(2):
                        sp.wait_ge(s_pj, NT * (NKV * b + NKV - 1 + s))
                        load(s, done)
                        done = done + 1
                for c in range(NCH):
                    if c < 2:
                        sp.wait_ge(s_pj, NT * (NKV * b + NKV + c + (-1 if last else 1)))
                    else:
                        sp.wait_ge(s_ff, 16 * b + NT * (c - 1))
                    load(NKV + c, done)
                    done = done + 1

            sequence(0, True, False)
            with sp.Fori(1, B - 1) as b:
                sequence(b, False, False)
            sequence(B - 1, False, True)
            store(B - 1)
            sp.wait_ge(s_stored, 16 * (B + 1))

        def expert_load(b, c, last):
            return 16 * (NS * b + NKV + c + (-1 if last else 1))

        @block.gpsimd
        def _(pool):
            nc.gpsimd.memset(half[:], 0.5).then_inc(s_stored, 16)

            def fetch(b):
                nc.gpsimd.tensor_copy(idx_cur[:], idx_all[:, bass.ds(b * NT, NT)]).then_inc(s_idx, 1)
                pool.wait_ge(s_idx, b + 1)
                stand_alone(pool, s_passed_pool)
                for t in range(NT):
                    nc.gpsimd.indirect_dma_start(
                        out=emb[:, t, :], out_offset=None, in_=table,
                        in_offset=bass.IndirectOffsetOnAxis(ap=idx_cur[:, t:t + 1], axis=0))\
                        .then_inc(s_gather, 16)

            def norm_root(e):
                pool.wait_ge(s_aggr, NT * (e + 1))
                stand_alone(pool, s_passed_pool)
                nc.gpsimd.tensor_scalar(std[:], mv[:, :, 1], LN_EPS, 1.0, ALU.add, ALU.mult)\
                    .then_inc(s_var, 1)
                pool.wait_ge(s_var, e + 1)
                nc.gpsimd.tensor_tensor(std[:], std[:], half[:, 0:NT], ALU.pow).then_inc(s_std, 1)

            def rotate_sum(n, t):
                pool.wait_ge(s_rope, NT * n + t + 1)
                nc.gpsimd.tensor_tensor(ropeA[:, t], ropeA[:, t], ropeB[:, t], ALU.add)\
                    .then_inc(s_radd, 1)

            def head_rms(n, pair):
                def rows(x):
                    return x[:, 2 * pair:2 * pair + 2].rearrange("p t c -> p (t c)")

                pool.wait_ge(s_sq, 12 * n + 6 * (pair + 1))
                nc.gpsimd.tensor_tensor(rows(rms), rows(ssq), half[:, 0:6], ALU.pow).then_inc(s_root, 1)
                pool.wait_ge(s_root, 2 * n + pair + 1)
                stand_alone(pool, s_passed_pool)
                nc.gpsimd.tensor_scalar(rows(rms), rows(rms), RMS_EPS, 1.0, ALU.add, ALU.mult)\
                    .then_inc(s_rms, 1)

            def norm_heads(n, t):
                if t % 2 == 0:
                    pool.wait_ge(s_rinv, 2 * n + t // 2 + 1)
                pool.wait_ge(s_radd, NT * n + t + 1)
                nc.gpsimd.tensor_tensor(ropeA[:, t], ropeA[:, t],
                                        rinv[:, t][:, :, None].to_broadcast([P, 3, HD]), ALU.mult)\
                    .then_inc(s_qkn, 1)

            def normalise(n, u):
                pool.wait_ge(s_rsum, U * n + u + 1)
                stand_alone(pool, s_passed_pool)
                w = (u % NT + 1) * P
                nc.gpsimd.tensor_scalar(prob[:, u % 4, 0:w], prob[:, u % 4, 0:w], rsum[:, u:u + 1],
                                        1.0, ALU.mult, ALU.mult).then_inc(s_prob, 1)

            def group(n, nxt=True, norm=None):
                for u in range(U):
                    if u + 2 < 6:
                        normalise(n, u + 2)
                    if not nxt:
                        continue
                    if u == 2:
                        head_rms(n + 1, 0)
                    if u == 3:
                        norm_heads(n + 1, 0)
                        norm_heads(n + 1, 1)
                        head_rms(n + 1, 1)
                    if u < NT:
                        rotate_sum(n + 1, u)
                if norm is not None:
                    norm_root(norm)
                if nxt:
                    norm_heads(n + 1, 2)
                    norm_heads(n + 1, 3)
                    normalise(n + 1, 0)
                    normalise(n + 1, 1)

            pool.wait_ge(s_const, 16 * CONSTS)
            fetch(0)
            norm_root(0)
            for t in range(NT):
                rotate_sum(0, t)
            head_rms(0, 0)
            head_rms(0, 1)
            for t in range(NT):
                norm_heads(0, t)
            normalise(0, 0)
            normalise(0, 1)
            group(0)
            with pool.Fori(0, B - 1) as b:
                n = NKV * b
                pool.wait_ge(s_emb, 2 * (b + 1))
                fetch(b + 1)
                with pool.Fori(1, NKV - 2) as g:
                    group(n + g)
                group(n + NKV - 2, norm=2 * b + 1)
                group(n + NKV - 1)
                group(n + NKV, norm=2 * b + 2)
            n = NKV * (B - 1)
            with pool.Fori(1, NKV - 1) as g:
                group(n + g)
            group(n + NKV - 1, nxt=False)
            norm_root(2 * B - 1)

        @block.scalar
        def _(act):
            copy = ACT.Copy

            def split_piece(i, k, dst):
                nc.scalar.activation(dst, prob[:, 2 * k:2 * k + 2, :].rearrange("p a n -> p (a n)"),
                                     copy).then_inc(s_split_hi, 1)

            act.wait_ge(s_const, 16 * CONSTS)
            nc.scalar.activation(gate_s[:, 0], gate_f[:], copy).then_inc(s_gatehi, 1)
            for q in range(WO_PIECES):
                act.wait_ge(s_stage[q % 2], 16 * (q // 2 + 1))
                split_piece(q, q % 2, wo_s[:, 0, 4 * q:4 * q + 4, :].rearrange("p a n -> p (a n)"))

            def slice_piece(i, s, j, k):
                act.wait_ge(s_stage[k], 16 * (WO_PIECES // 2 + j + 1))
                if not (isinstance(i, int) and i < 2):
                    act.wait_ge(s_wstore[k], 16 * j)
                split_piece(i, k, W[:, k, 0].rearrange("p k n -> p (k n)"))
                act.wait_ge(s_split_hi, WO_PIECES + i + 1)
                act.wait_ge(s_split_lo, WO_PIECES + i + 1)
                act.dma_start(w_split[bass.ds(s, 1)].rearrange("a p n -> p (a n)"),
                              W[:, k].rearrange("p a k n -> p (a k n)").bitcast(F32)).then_inc(s_wstore[k], 16)

            for k in range(2):
                slice_piece(k, k + 2, 0, k)
            with act.Fori(1, SLICE_STEPS // 2) as j:
                for k in range(2):
                    slice_piece(2 * j + k, 2 * j + k + 2, j, k)
            for k in range(2):
                slice_piece(SLICE_STEPS + k, k, SLICE_STEPS // 2, k)

            def lora_copy(b):
                act.wait_ge(s_loraT, b + 1)
                nc.scalar.activation(loraT[:], ov[0:R, :], copy).then_inc(s_loraC, 1)

            def normed_hi(e, which, tiles=range(NT)):
                for t in tiles:
                    act.wait_ge(s_xt, NT * e + t + 1)
                    nc.scalar.activation(lnT[which][:, 0, :, t * P:(t + 1) * P], tp[t % 2][:, 0:KC, :],
                                         copy).then_inc(s_xh, 1)

            def squares(n, t):
                act.wait_ge(s_pj, NT * n + t + 1)
                for c in range(3):
                    wait_past(act, s_sq, 12 * n + 3 * t + c - 3)
                    nc.scalar.activation(sq_junk[:, (3 * t + c) % 4], pj[t % 2][:, c * HD:(c + 1) * HD],
                                         ACT.Square, scale=float(HD) ** -0.5,
                                         accum_out=ssq[:, t, c:c + 1]).then_inc(s_sq, 1)
                if t == 0:
                    wait_past(act, s_vl, n)
                nc.scalar.activation(vraw[:, t], pj[t % 2][:, 3 * HD:], copy).then_inc(s_vraw, 1)

            def queries_hi(n, t):
                act.wait_ge(s_qkT, NT * n + t + 1)
                nc.scalar.activation(qkT[:, 0, :, t * P:(t + 1) * P], tp[t % 2][:, 0:3, :], copy)\
                    .then_inc(s_qkh, 1)

            def values_hi(n):
                act.wait_ge(s_vraw, NT * (n + 1))
                nc.scalar.activation(V[:, 0], vraw[:], copy).then_inc(s_vh, 1)

            def exponential(n, u):
                act.wait_ge(s_bias, U * n + u + 1)
                w = (u % NT + 1) * P
                nc.scalar.activation(prob[:, u % 4, 0:w], sc[u % 2][:, 0:w], ACT.Exp,
                                     bias=nbias[:, u:u + 1],
                                     accum_out=rowsum[:, u:u + 1]).then_inc(s_exp, 1)

            def normalise(n, u):
                act.wait_ge(s_rsum, U * n + u + 1)
                w = (u % NT + 1) * P
                nc.scalar.activation(prob[:, u % 4, 0:w], prob[:, u % 4, 0:w], copy,
                                     scale=rsum[:, u:u + 1]).then_inc(s_prob_late, 1)

            def probs_hi(n, u):
                act.wait_ge(s_pT, U * n + u + 1)
                t = u % NT
                nc.scalar.activation(pT[:, u // NT, 0, 0:t + 1, t * P:(t + 1) * P],
                                     tp[u % 2][:, 0:t + 1, :], copy).then_inc(s_pTh, 1)

            def heads_hi(n, r):
                act.wait_ge(s_pv, REP * n + r + 1)
                nc.scalar.activation(yT[:, r, 0], ov[:], copy).then_inc(s_yh, 1)

            def expert_odds(b):
                act.wait_ge(s_gdiff, b + 1)
                nc.scalar.activation(gexp[:], gdiff[:], ACT.Exp).then_inc(s_gexp, 1)

            def group(n, carry=True, nxt=True, embed=None, finish=None):
                def norm_hi(t):
                    if embed is not None:
                        normed_hi(2 * embed - 1, 0, [t])
                    if finish is not None:
                        normed_hi(2 * finish + 2, 1, [t])

                for u in range(U):
                    if u == 0 and embed is not None:
                        lora_copy(embed)
                    if u < NT and nxt:
                        squares(n + 1, u)
                    if u == 5:
                        normalise(n, 6)
                    if u == 6:
                        if nxt:
                            queries_hi(n + 1, 1)
                        normalise(n, 7)
                    probs_hi(n, u)
                    if u == 5 and nxt:
                        queries_hi(n + 1, 0)
                    if u + 2 < U:
                        exponential(n, u + 2)
                if carry:
                    act.wait_ge(s_op, 2 * n)
                heads_hi(n, 0)
                if nxt:
                    exponential(n + 1, 0)
                    exponential(n + 1, 1)
                    queries_hi(n + 1, 2)
                    queries_hi(n + 1, 3)
                    for t in range(NT):
                        norm_hi(t)
                heads_hi(n, 1)
                if nxt:
                    values_hi(n + 1)
                if finish is not None:
                    expert_odds(finish)

            lora_copy(0)
            normed_hi(0, 0)
            for t in range(NT):
                squares(0, t)
            values_hi(0)
            for t in range(NT):
                queries_hi(0, t)
            exponential(0, 0)
            exponential(0, 1)
            group(0, carry=False)
            with act.Fori(0, B - 1) as b:
                n = NKV * b
                with act.Fori(1, NKV - 2) as g:
                    group(n + g)
                group(n + NKV - 2, embed=b + 1)
                group(n + NKV - 1)
                group(n + NKV, carry=False, finish=b)
            n = NKV * (B - 1)
            with act.Fori(1, NKV - 1) as g:
                group(n + g)
            group(n + NKV - 1, nxt=False)
            normed_hi(2 * B - 1, 1)
            expert_odds(B - 1)

        @block.vector
        def _(dve):
            def raw(x):
                return x.bitcast(F32)

            dve.wait_ge(s_const, 16 * CONSTS)
            nc.vector.tensor_scalar(norm_in[:, 0], norm_in[:, 0], ATT_SCALE, None, ALU.mult)\
                .then_inc(s_tab, 1)
            dve.wait_ge(s_tab, 1)
            for c in range(3):
                wsel = norm_in[:, 0 if c < 2 else 1]
                for t in range(NT):
                    nc.vector.tensor_tensor(tabA[:, t, c].rearrange("p (a d) -> p a d", a=2), wsel,
                                            cs[:, 0, t][:, None, :].to_broadcast([P, 2, HD // 2]),
                                            ALU.mult)
                    nc.vector.tensor_tensor(tabB[:, t, c, HD // 2:], wsel[:, 0], cs[:, 1, t], ALU.mult)
                    nc.vector.scalar_tensor_tensor(tabB[:, t, c, 0:HD // 2], wsel[:, 1], -1.0,
                                                   cs[:, 1, t], ALU.mult, ALU.mult).then_inc(s_tab, 1)
            nc.vector.tensor_copy(ident_b[:], ident_f[:])
            nc.vector.tensor_copy(mask_b[:], mask_f[:]).then_inc(s_tab, 1)
            dve.wait_ge(s_tab, TABS)
            dve.wait_ge(s_gatehi, 1)
            nc.vector.tensor_tensor(gate_s[:, 1], gate_f[:], raw(gate_s[:, 0]), ALU.subtract)\
                .then_inc(s_tab, 1)

            def split_piece(i, k, hi, lo):
                dve.wait_ge(s_split_hi, i + 1)
                nc.vector.tensor_tensor(lo, prob[:, 2 * k:2 * k + 2, :].rearrange("p a n -> p (a n)"),
                                        raw(hi), ALU.subtract).then_inc(s_split_lo, 1)

            for q in range(WO_PIECES):
                hi, lo = (wo_s[:, x, 4 * q:4 * q + 4, :].rearrange("p a n -> p (a n)") for x in range(2))
                split_piece(q, q % 2, hi, lo)

            def slice_piece(i, k):
                hi, lo = (W[:, k, x].rearrange("p k n -> p (k n)") for x in range(2))
                split_piece(WO_PIECES + i, k, hi, lo)

            with dve.Fori(0, NS // 2) as j:
                for k in range(2):
                    slice_piece(2 * j + k, k)

            def embed(b, pairs=range(2)):
                wait_past(dve, s_stored, 16 * b)
                for pair in pairs:
                    dve.wait_ge(s_loraM, 2 * b + pair + 1)
                    bank = op[:] if pair == 0 else ov[:].rearrange("p (t d) -> p t d", t=2)
                    nc.vector.scalar_tensor_tensor(
                        h[:, bass.ds(b % 2, 1), 2 * pair:2 * pair + 2].rearrange("p a t d -> p (a t) d"),
                        bank, LORA_SCALING, emb[:, 2 * pair:2 * pair + 2, 0:D], ALU.mult, ALU.add)\
                        .then_inc(s_emb, 1)

            def h_tile(b, t):
                return h[:, bass.ds(b % 2, 1), t].rearrange("p a d -> p (a d)")

            def norm_stats(e, b):
                stand_alone(dve, s_passed_dve)
                for t in range(NT):
                    nc.vector.bn_stats(stats[:, t], h_tile(b, t)).then_inc(s_stat, 1)
                for t in range(NT):
                    dve.wait_ge(s_stat, NT * e + t + 1)
                    stand_alone(dve, s_passed_dve)
                    nc.vector.bn_aggr(mv[:, t], stats[:, t]).then_inc(s_aggr, 1)

            def norm_apply(e, b, tiles=range(NT)):
                if 0 in tiles:
                    dve.wait_ge(s_std, e + 1)
                    nc.vector.reciprocal(rstd[:], std[:]).then_inc(s_rstd, 1)
                    dve.wait_ge(s_rstd, e + 1)
                for t in tiles:
                    nc.vector.tensor_scalar(xn[:, t], h_tile(b, t), mv[:, t, 0:1], rstd[:, t:t + 1],
                                            ALU.subtract, ALU.mult).then_inc(s_xn, 1)

            def normed_lo(e, which, tiles=range(NT)):
                for t in tiles:
                    dve.wait_ge(s_xh, NT * e + t + 1)
                    cols = slice(t * P, (t + 1) * P)
                    nc.vector.tensor_tensor(lnT[which][:, 1, :, cols], tp[t % 2][:, 0:KC, :],
                                            raw(lnT[which][:, 0, :, cols]), ALU.subtract)\
                        .then_inc(s_xl, 1)

            def rotate(n, t):
                dve.wait_ge(s_vraw, NT * n + t + 1)
                wait_past(dve, s_qkT, NT * (n - 1) + t + 1)
                qk = pj[t % 2][:, 0:3 * HD]
                nc.vector.tensor_tensor(ropeA[:, t], qk.rearrange("p (c d) -> p c d", c=3), tabA[:, t],
                                        ALU.mult)
                nc.vector.tensor_tensor(
                    ropeB[:, t].rearrange("p c (a d) -> p c a d", a=2),
                    qk.rearrange("p (c a d) -> p c a d", c=3, a=2)[:, :, ::-1, :],
                    tabB[:, t].rearrange("p c (a d) -> p c a d", a=2), ALU.mult).then_inc(s_rope, 1)

            def norm_factors(n, pair):
                dve.wait_ge(s_rms, 2 * n + pair + 1)
                nc.vector.reciprocal(rinv[:, 2 * pair:2 * pair + 2], rms[:, 2 * pair:2 * pair + 2])\
                    .then_inc(s_rinv, 1)

            def queries_lo(n, t):
                dve.wait_ge(s_qkh, NT * n + t + 1)
                cols = slice(t * P, (t + 1) * P)
                nc.vector.tensor_tensor(qkT[:, 1, :, cols], tp[t % 2][:, 0:3, :],
                                        raw(qkT[:, 0, :, cols]), ALU.subtract).then_inc(s_qkl, 1)

            def values_lo(n):
                dve.wait_ge(s_vh, n + 1)
                nc.vector.tensor_tensor(V[:, 1], vraw[:], raw(V[:, 0]), ALU.subtract).then_inc(s_vl, 1)

            def maximum(n, u):
                dve.wait_ge(s_score, U * n + u + 1)
                nc.vector.tensor_reduce(nbias[:, u:u + 1], sc[u % 2][:, 0:(u % NT + 1) * P], AX,
                                        ALU.max, negate=True).then_inc(s_bias, 1)

            def inverse_sum(n, u):
                dve.wait_ge(s_exp, U * n + u + 1)
                nc.vector.reciprocal(rsum[:, u:u + 1], rowsum[:, u:u + 1]).then_inc(s_rsum, 1)

            def probs_lo(n, u):
                dve.wait_ge(s_pTh, U * n + u + 1)
                r, t = u // NT, u % NT
                cols = slice(t * P, (t + 1) * P)
                nc.vector.tensor_tensor(pT[:, r, 1, 0:t + 1, cols], tp[u % 2][:, 0:t + 1, :],
                                        raw(pT[:, r, 0, 0:t + 1, cols]), ALU.subtract)\
                    .then_inc(s_pTl, 1)

            def heads_lo(n, r):
                dve.wait_ge(s_yh, REP * n + r + 1)
                nc.vector.tensor_tensor(yT[:, r, 1], ov[:], raw(yT[:, r, 0]), ALU.subtract)\
                    .then_inc(s_yl, 1)

            def add_attention(n, b, pair):
                dve.wait_ge(s_op, 2 * n + pair + 1)
                dst = h[:, bass.ds(b % 2, 1), 2 * pair:2 * pair + 2].rearrange("p a t d -> p (a t) d")
                nc.vector.tensor_tensor(dst, op[:], dst, ALU.add).then_inc(s_hadd, 1)

            def router(b):
                k = [6 * b]

                def step(ins):
                    k[0] = k[0] + 1
                    ins.then_inc(s_rt, 1)
                    dve.wait_ge(s_rt, k[0])

                dve.wait_ge(s_gate, b + 1)
                step(nc.vector.tensor_copy(logits[:].rearrange("p t e -> p (t e)"), op[:, 0, 0:NT * NE]))
                stand_alone(dve, s_passed_dve)
                for t in range(NT):
                    last = nc.vector.max(top8[:, t], logits[:, t])
                step(last)
                nc.vector.tensor_tensor(gdiff[:], top8[:, :, 1], top8[:, :, 0], ALU.subtract)\
                    .then_inc(s_gdiff, 1)
                stand_alone(dve, s_passed_dve)
                for t in range(NT):
                    last = nc.vector.max_index(top8i[:, t], top8[:, t], logits[:, t])
                step(last)
                step(nc.vector.tensor_copy(topf[:], top8i[:, :, 0:2]))
                for i in range(2):
                    nc.vector.tensor_tensor(hot[:, i], iota_e[:][:, None, :].to_broadcast([P, NT, NE]),
                                            topf[:, :, i:i + 1].to_broadcast([P, NT, NE]), ALU.is_equal)
                dve.wait_ge(s_gexp, b + 1)
                step(nc.vector.tensor_scalar(gden[:], gexp[:], 1.0, None, ALU.add))
                step(nc.vector.reciprocal(gw[:, 0], gden[:]))

            def router_weights(b):
                k = 3 * b
                nc.vector.tensor_tensor(gw[:, 1], gw[:, 0], gexp[:], ALU.mult).then_inc(s_rw, 1)
                dve.wait_ge(s_rw, k + 1)
                for i in range(2):
                    last = nc.vector.tensor_tensor(hot[:, i], hot[:, i],
                                                   gw[:, i][:, :, None].to_broadcast([P, NT, NE]), ALU.mult)
                last.then_inc(s_rw, 1)
                dve.wait_ge(s_rw, k + 2)
                nc.vector.tensor_tensor(wfull[:], hot[:, 0], hot[:, 1], ALU.add).then_inc(s_rw, 1)
                dve.wait_ge(s_rw, k + 3)

            def experts(b):
                for f in range(NCH * NT):
                    c, t = divmod(f, NT)
                    dve.wait_ge(s_ff, 16 * b + f + 1)
                    for i in range(EPC):
                        if i:
                            dve.wait_ge(s_ffc, 32 * b + 2 * f + 1)
                        e = EPC * c + i
                        nc.vector.scalar_tensor_tensor(h_tile(b, t), pj[f % 2][:, i * D:(i + 1) * D],
                                                       wfull[:, t, e:e + 1], h_tile(b, t),
                                                       ALU.mult, ALU.add).then_inc(s_ffc, 1)

            def group(n, b, carry=True, nxt=True, embed_next=False, finish=None):
                norm = 2 * b + 1 if embed_next else 2 * finish + 2 if finish is not None else None
                nb = b + 1 if embed_next else finish

                def norm_lo(t):
                    if norm is not None:
                        normed_lo(norm, 0 if embed_next else 1, [t])

                for u in range(U):
                    if u == 5 and carry:
                        add_attention(n - 1, b, 0)
                    if u in (2, 4) and finish is not None:
                        add_attention(n - 1, finish, u // 2 - 1)
                    if u + 2 < U:
                        maximum(n, u + 2)
                    if u < 2 and nxt:
                        rotate(n + 1, u)
                    if u == 6 and nxt:
                        queries_lo(n + 1, 1)
                    probs_lo(n, u)
                    if 2 <= u < NT and nxt:
                        rotate(n + 1, u)
                    if u == 5 and nxt:
                        queries_lo(n + 1, 0)
                    if u + 2 < U:
                        inverse_sum(n, u + 2)
                    if u in (3, 5) and nxt:
                        norm_factors(n + 1, (u - 3) // 2)
                    if u in (1, 3) and embed_next:
                        embed(nb, [u // 2])
                    if u == 4 and norm is not None:
                        if embed_next:
                            dve.wait_ge(s_emb, 2 * (nb + 1))
                        else:
                            dve.wait_ge(s_hadd, 1 + 2 * n)
                        norm_stats(norm, nb)
                if norm is not None:
                    norm_apply(norm, nb, range(2))
                if nxt:
                    maximum(n + 1, 0)
                heads_lo(n, 0)
                if nxt:
                    maximum(n + 1, 1)
                if norm is not None:
                    norm_apply(norm, nb, range(2, NT))
                if carry:
                    add_attention(n - 1, b, 1)
                if nxt:
                    inverse_sum(n + 1, 0)
                    inverse_sum(n + 1, 1)
                    queries_lo(n + 1, 2)
                    queries_lo(n + 1, 3)
                for t in range(NT):
                    norm_lo(t)
                heads_lo(n, 1)
                if nxt:
                    values_lo(n + 1)
                if finish is not None:
                    router(finish)
                    router_weights(finish)
                    experts(finish)

            dve.sem_inc(s_hadd, 1)
            embed(0)
            dve.wait_ge(s_emb, 2)
            norm_stats(0, 0)
            norm_apply(0, 0)
            normed_lo(0, 0)
            for t in range(NT):
                rotate(0, t)
            for pair in range(2):
                norm_factors(0, pair)
            values_lo(0)
            for t in range(NT):
                queries_lo(0, t)
            maximum(0, 0)
            maximum(0, 1)
            inverse_sum(0, 0)
            inverse_sum(0, 1)
            group(0, 0, carry=False)
            with dve.Fori(0, B - 1) as b:
                n = NKV * b
                with dve.Fori(1, NKV - 2) as g:
                    group(n + g, b)
                group(n + NKV - 2, b, embed_next=True)
                group(n + NKV - 1, b)
                group(n + NKV, b + 1, carry=False, finish=b)
            b = B - 1
            n = NKV * b
            with dve.Fori(1, NKV - 1) as g:
                group(n + g, b)
            n = n + NKV - 1
            group(n, b, nxt=False)
            for pair in range(2):
                add_attention(n, b, pair)
            dve.wait_ge(s_hadd, 1 + 2 * (n + 1))
            norm_stats(2 * B - 1, b)
            norm_apply(2 * B - 1, b)
            normed_lo(2 * B - 1, 1)
            router(b)
            router_weights(b)
            experts(b)

        @block.tensor
        def _(pe):
            mm = nc.tensor.matmul

            def three_pass(dst, lhs, rhs, start, stop):
                mm(dst, lhs[0], rhs[0], start=start, stop=False)
                mm(dst, lhs[0], rhs[1], start=False, stop=False)
                return mm(dst, lhs[1], rhs[0], start=False, stop=stop)

            def lora_transpose(b, n):
                pe.wait_ge(s_gather, 64 * (b + 1))
                wait_past(pe, s_yl, REP * n)
                for t in range(NT):
                    last = nc.tensor.transpose(ov[0:R, t * P:(t + 1) * P], emb[:, t, D:D + R], ident_f[:])
                last.then_inc(s_loraT, 1)

            def lora_product(b, n):
                pe.wait_ge(s_loraC, b + 1)
                wait_past(pe, s_hadd, 2 * n - 1)
                for pair in range(2):
                    bank = op[:] if pair == 0 else ov[:].rearrange("p (t d) -> p t d", t=2)
                    for i in range(2):
                        t = 2 * pair + i
                        last = mm(bank[:, i], loraT[:, t * P:(t + 1) * P], loraB[:], start=True, stop=True)
                    last.then_inc(s_loraM, 1)

            def norm_transpose(e, t, before=None):
                pe.wait_ge(s_xn, NT * e + t + 1)
                if before is not None:
                    pe.wait_ge(*before)
                elif t >= 2:
                    pe.wait_ge(s_xl, NT * e + t - 1)
                for k in range(KC):
                    last = nc.tensor.transpose(tp[t % 2][:, k], xn[:, t, k * P:(k + 1) * P], ident_f[:])
                last.then_inc(s_xt, 1)

            def project(n, t, slot, bank_free):
                for s, v in bank_free:
                    wait_past(pe, s, v)
                for k in range(KC):
                    last = three_pass(pj[t % 2][:], [lnT[0][:, x, k, t * P:(t + 1) * P] for x in range(2)],
                                      [W[:, bass.ds(slot, 1), x, k, :].rearrange("p a n -> p (a n)")
                                       for x in range(2)], start=k == 0, stop=k == KC - 1)
                last.then_inc(s_pj, 1)

            def bank_read(n, t):
                return [(s_rope, NT * n + t + 1), (s_vraw, NT * n + t + 1)]

            def qk_transpose(n, t, before):
                pe.wait_ge(s_qkn, NT * n + t + 1)
                wait_past(pe, *before)
                for c in range(3):
                    last = nc.tensor.transpose(tp[t % 2][:, c], ropeA[:, t, c], ident_f[:])
                last.then_inc(s_qkT, 1)

            def score(n, u):
                r, t = u // NT, u % NT
                pe.wait_ge(s_qkl, NT * n + t + 1)
                w = (t + 1) * P
                if u >= 2:
                    pe.wait_ge(s_exp, U * n + u - 1)
                else:
                    wait_past(pe, s_exp, U * (n - 1) + u + 7)
                three_pass(sc[u % 2][:, 0:w], [qkT[:, x, r, t * P:(t + 1) * P] for x in range(2)],
                           [qkT[:, x, 2, 0:w] for x in range(2)], start=True, stop=False)
                mm(sc[u % 2][:, t * P:w], ident_b[:], mask_b[:], start=False, stop=True)\
                    .then_inc(s_score, 1)

            def prob_transpose(n, u, before):
                if u < 6:
                    pe.wait_ge(s_prob, 6 * n + u + 1)
                else:
                    pe.wait_ge(s_prob_late, 2 * n + u - 5)
                wait_past(pe, *before)
                for kt in range(u % NT + 1):
                    last = nc.tensor.transpose(tp[u % 2][:, kt], prob[:, u % 4, kt * P:(kt + 1) * P],
                                               ident_f[:])
                last.then_inc(s_pT, 1)

            def value_product(n, r):
                pe.wait_ge(s_pTl, U * n + NT * (r + 1))
                if r == 0:
                    pe.wait_ge(s_vl, n + 1)
                else:
                    pe.wait_ge(s_yl, REP * n + r)
                for kt in range(NT):
                    last = three_pass(ov[:, kt * P:], [V[:, x, kt] for x in range(2)],
                                      [pT[:, r, x, kt, kt * P:] for x in range(2)],
                                      start=kt == 0, stop=kt == NT - 1)
                last.then_inc(s_pv, 1)

            def output_product(n, g, pair):
                pe.wait_ge(s_yl, REP * (n + 1))
                pe.wait_ge(s_hadd, 2 * n + 1 + pair)
                for i in range(2):
                    t = 2 * pair + i
                    for r in range(REP):
                        last = three_pass(
                            op[:, i], [yT[:, r, x, t * P:(t + 1) * P] for x in range(2)],
                            [wo_s[:, x, bass.ds(REP * g + r, 1), :].rearrange("p a d -> p (a d)")
                             for x in range(2)], start=r == 0, stop=r == REP - 1)
                last.then_inc(s_op, 1)

            def group(n, b, g, carry=True, nxt=True, embed=None, finish=None, fresh=None):
                norm = 2 * embed - 1 if embed is not None else 2 * finish + 2 if finish is not None else None

                def unit_read(u):
                    return s_pTl, U * n + u + 1

                def keys_read(m, t):
                    return s_qkl, NT * m + t + 1

                def norm_read(e, t):
                    return s_xl, NT * e + t + 1

                for u in range(U):
                    if u < NT and nxt:
                        if u == 0 and finish is None:
                            if not (isinstance(n, int) and n == 0):
                                pe.wait_ge(s_wload, 16 * (NS * b + g))
                        elif u == 0:
                            pe.wait_ge(s_wload, 16 * (NS * finish + NKV))
                        if fresh is not None:
                            pe.wait_ge(*norm_read(fresh, u))
                        project(n + 1, u, (g + 1) % 2,
                                bank_read(n, u + 2) if u < 2 else bank_read(n + 1, u - 2))
                    if embed is not None:
                        if u == 0:
                            lora_transpose(embed, n)
                        if u == 1:
                            lora_product(embed, n)
                    if finish is not None and u in (1, 3):
                        output_product(n - 1, NKV - 1, u // 2)
                    if carry and u == 4:
                        if embed is not None:
                            pe.wait_ge(s_emb, 2 * embed + 1)
                        output_product(n - 1, g - 1, 0)
                    if u == 5:
                        if embed is not None:
                            pe.wait_ge(s_emb, 2 * (embed + 1))
                        value_product(n, 0)
                    if u == 6:
                        if nxt:
                            qk_transpose(n + 1, 0, unit_read(4))
                            qk_transpose(n + 1, 1, unit_read(5))
                        if carry:
                            output_product(n - 1, g - 1, 1)
                    if u < 2:
                        if fresh is not None:
                            pe.wait_ge(*norm_read(fresh, u + 2))
                        before = keys_read(n, u + 2)
                    elif u < 6 or not nxt:
                        before = unit_read(u - 2)
                    else:
                        before = keys_read(n + 1, u - 6)
                    prob_transpose(n, u, before)
                    if u + 2 < U:
                        score(n, u + 2)
                if nxt:
                    for t in range(2):
                        score(n + 1, t)
                    for t in range(2, NT):
                        qk_transpose(n + 1, t, unit_read(4 + t))
                    if norm is not None:
                        for t in range(NT):
                            norm_transpose(norm, t, keys_read(n + 1, 2 + t) if t < 2 else None)
                value_product(n, 1)
                if finish is not None:
                    router_product(norm)

            def router_product(e):
                pe.wait_ge(s_xl, NT * (e + 1))
                for t in range(NT):
                    for k in range(KC):
                        last = three_pass(op[:, 0, t * NE:(t + 1) * NE],
                                          [lnT[1][:, x, k, t * P:(t + 1) * P] for x in range(2)],
                                          [gate_s[:, x, k * NE:(k + 1) * NE] for x in range(2)],
                                          start=k == 0, stop=k == KC - 1)
                last.then_inc(s_gate, 1)

            def experts(b, n, last):
                for f in range(NCH * NT):
                    c, t = divmod(f, NT)
                    if t == 0:
                        pe.wait_ge(s_wload, expert_load(b, c, last))
                    if f < 2:
                        for s, v in bank_read(n, f + 2):
                            pe.wait_ge(s, v)
                    else:
                        pe.wait_ge(s_ffc, 32 * b + 2 * (f - 1))
                    for k in range(KC):
                        last_mm = three_pass(pj[f % 2][:],
                                             [lnT[1][:, x, k, t * P:(t + 1) * P] for x in range(2)],
                                             [W[:, c % 2, x, k, :] for x in range(2)],
                                             start=k == 0, stop=k == KC - 1)
                    last_mm.then_inc(s_ff, 1)

            pe.wait_ge(s_const, 16 * CONSTS)
            pe.wait_ge(s_tab, TABS + 1)
            lora_transpose(0, 0)
            lora_product(0, 0)
            for t in range(NT):
                norm_transpose(0, t)
            pe.wait_ge(s_split_lo, WO_PIECES + NS)
            for t in range(NT):
                pe.wait_ge(s_xl, t + 1)
                project(0, t, 0, [] if t < 2 else bank_read(0, t - 2))
            for t in range(NT):
                qk_transpose(0, t, (s_xl, 3 + t) if t < 2 else (s_qkl, t - 1))
            score(0, 0)
            score(0, 1)
            pe.wait_ge(s_emb, 2)
            group(0, 0, 0, carry=False)
            with pe.Fori(0, B - 1) as b:
                n = NKV * b
                with pe.Fori(1, NKV - 2) as g:
                    group(n + g, b, g)
                group(n + NKV - 2, b, NKV - 2, embed=b + 1)
                group(n + NKV - 1, b, NKV - 1, fresh=2 * b + 1)
                group(n + NKV, b + 1, 0, carry=False, finish=b)
                experts(b, n + NKV + 1, False)
                pe.wait_ge(s_ffc, 32 * (b + 1))
            b = B - 1
            n = NKV * b
            with pe.Fori(1, NKV - 1) as g:
                group(n + g, b, g)
            n = n + NKV - 1
            group(n, b, NKV - 1, nxt=False)
            for pair in range(2):
                output_product(n, NKV - 1, pair)
            for t in range(NT):
                norm_transpose(2 * B - 1, t, (s_pTl, U * n + 7 + t) if t < 2 else None)
            router_product(2 * B - 1)
            experts(b, n, True)


def kernel(**inputs):
    import numpy as np
    import concourse.bacc as bacc
    from concourse.bass_utils import run_bass_kernel_spmd

    def arr(name):
        return np.asarray(inputs[name])

    table = np.concatenate([arr("L0_tok_emb_weight"), arr("L0_tok_lora_A").T], axis=1)
    ids = np.ascontiguousarray(arr("x").reshape(B * NT, P).T)
    def halves(w):
        return w.reshape(w.shape[0], -1, HD // 2, 2).transpose(0, 1, 3, 2).reshape(w.shape[0], -1, HD)

    wq = halves(arr("L0_attn_wq")).reshape(D, NKV, REP * HD)
    wk = halves(arr("L0_attn_wk"))
    wv = arr("L0_attn_wv").reshape(D, NKV, HD)
    qkv = np.concatenate([wq, wk, wv], axis=2).transpose(1, 0, 2)
    ew = arr("L0_ffn_expert_w").reshape(NCH, EPC * D, D).transpose(0, 2, 1)
    w_slices = np.concatenate([qkv, ew]).reshape(NS, KC, P, 512).transpose(0, 2, 1, 3)
    wo = arr("L0_attn_wo").reshape(NH, HD, D).transpose(1, 0, 2).reshape(HD, NH * D)
    gate = arr("L0_ffn_gate_w").T.reshape(KC, P, NE).transpose(1, 0, 2).reshape(P, KC * NE)
    norms = np.stack([arr("L0_attn_q_norm_w"), arr("L0_attn_k_norm_w")]).reshape(2, HD // 2, 2)
    norms = np.broadcast_to(norms.transpose(0, 2, 1), (P, 2, 2, HD // 2))
    theta = np.float32(1e6) ** (np.float32(-2.0) * np.arange(HD // 2, dtype=np.float32) / np.float32(HD))
    angle = np.arange(T, dtype=np.float32)[:, None] * theta[None, :].astype(np.float32)
    rope = np.stack([np.cos(angle), np.sin(angle)]).astype(np.float32)
    rope = rope.reshape(2, NT, P, HD // 2).transpose(2, 0, 1, 3)
    mask = np.triu(np.full((P, P), -3e37, np.float32), k=1)
    data = {
        "ids": ids, "table": table, "lora_b": arr("L0_tok_lora_B").T,
        "w_slices": w_slices.reshape(NS, P, SL), "wo": wo, "gate": gate, "norm_w": norms, "rope": rope,
        "ident": np.eye(P, dtype=np.float32), "mask": mask,
        "iota": np.broadcast_to(np.arange(NE, dtype=np.float32), (P, NE)),
    }
    nc = bacc.Bacc("TRN2", target_bir_lowering=False, num_devices=1)
    arrays, args = {}, {}
    for name, a in data.items():
        a = np.ascontiguousarray(a)
        arrays[f"in_{name}"] = a
        args[name] = nc.dram_tensor(f"in_{name}", a.shape, mybir.dt.from_np(a.dtype),
                                    kind="ExternalInput").ap()
    args["out"] = nc.dram_tensor("out_h", (B, T, D), F32, kind="ExternalOutput").ap()
    build_tower(nc, **args)
    r = run_bass_kernel_spmd(nc, [arrays], core_ids=[0])
    return r.results[0]["out_h"]
```

```python
from contextlib import ExitStack

import concourse.bass as bass
from concourse import mybir

F32 = mybir.dt.float32
F32R = mybir.dt.float32r
BF16 = mybir.dt.bfloat16
I32 = mybir.dt.int32
U32 = mybir.dt.uint32
ALU = mybir.AluOpType
ACT = mybir.ActivationFunctionType
AX = mybir.AxisListType.X

B, T, D = 8, 512, 256
R = 16
LORA_SCALING = 2.0
HD, NH, NKV = 128, 16, 8
REP = NH // NKV
NE = 8
P = 128
NT = T // P
KC = D // P
U = REP * NT
EPC = 2
NCH = NE // EPC
NS = NKV + NCH
SL = KC * 512
ATT_SCALE = float(HD) ** -0.5
RMS_EPS = 1e-6
LN_EPS = 1e-5


def wait_past(eng, sem, value):
    if not (isinstance(value, int) and value <= 0):
        eng.wait_ge(sem, value)


def stand_alone(eng, s_passed):
    eng.sem_inc(s_passed, 1)


def build_tower(nc, ids, table, lora_b, w_slices, wo, gate, norm_w, rope, ident, mask, iota, out):
    ctx = ExitStack()
    with ctx:
        def sb(name, shape, dt=F32):
            return ctx.enter_context(nc.sbuf_tensor(name, shape, dt))

        def pb(name, shape, dt=F32):
            return ctx.enter_context(nc.psum_tensor(name, shape, dt))

        def sem(name):
            return ctx.enter_context(nc.semaphore(name))

        w_split = nc.dram_tensor("w_split", (NS, P, 2 * SL), F32, kind="Internal").ap()

        ident_f = sb("ident_f", [P, P])
        ident_b = sb("ident_b", [P, P], BF16)
        mask_b = sb("mask_b", [P, P], BF16)
        mask_f = sb("mask_f", [P, P])
        iota_e = sb("iota_e", [P, NE])
        half = sb("half", [P, 6])
        idx_all = sb("idx_all", [P, B * NT], I32)
        idx_cur = sb("idx_cur", [P, NT], I32)
        loraB = sb("loraB", [R, D])
        loraT = sb("loraT", [R, T])
        emb = sb("emb", [P, NT, D + R])
        h = sb("h", [P, 2, NT, D])
        norm_in = sb("norm_in", [P, 2, 2, HD // 2])
        cs = sb("cs", [P, 2, NT, HD // 2])
        tabA = sb("tabA", [P, NT, 3, HD])
        tabB = sb("tabB", [P, NT, 3, HD])
        W = sb("W", [P, 2, 2, KC, 512], F32R)
        wo_s = sb("wo_s", [P, 2, NH, D], F32R)
        gate_f = sb("gate_f", [P, KC * NE])
        gate_s = sb("gate_s", [P, 2, KC * NE], F32R)
        xn = sb("xn", [P, NT, D])
        lnT = [sb(f"ln{i}T", [P, 2, KC, T], F32R) for i in (1, 2)]
        stats = sb("stats", [P, NT, 6])
        mv = sb("mv", [P, NT, 2])
        std = sb("std", [P, NT])
        rstd = sb("rstd", [P, NT])
        sq_junk = sb("sq_junk", [P, 4, HD])
        ssq = sb("ssq", [P, NT, 3])
        rms = sb("rms", [P, NT, 3])
        rinv = sb("rinv", [P, NT, 3])
        ropeA = sb("ropeA", [P, NT, 3, HD])
        ropeB = sb("ropeB", [P, NT, 3, HD])
        vraw = sb("vraw", [P, NT, HD])
        V = sb("V", [P, 2, NT, HD], F32R)
        qkT = sb("qkT", [P, 2, 3, T], F32R)
        nbias = sb("nbias", [P, U])
        rowsum = sb("rowsum", [P, U])
        rsum = sb("rsum", [P, U])
        prob = sb("prob", [P, 4, T])
        pT = sb("pT", [P, REP, 2, NT, T], F32R)
        yT = sb("yT", [P, REP, 2, T], F32R)
        logits = sb("logits", [P, NT, NE])
        top8 = sb("top8", [P, NT, 8])
        top8i = sb("top8i", [P, NT, 8], U32)
        topf = sb("topf", [P, NT, 2])
        gdiff = sb("gdiff", [P, NT])
        gexp = sb("gexp", [P, NT])
        gden = sb("gden", [P, NT])
        gw = sb("gw", [P, 2, NT])
        hot = sb("hot", [P, 2, NT, NE])
        wfull = sb("wfull", [P, NT, NE])

        pj = [pb(f"pj{i}", [P, 512]) for i in range(2)]
        tp = [pb(f"tp{i}", [P, NT, P]) for i in range(2)]
        sc = [pb(f"sc{i}", [P, T]) for i in range(2)]
        ov = pb("ov", [P, T])
        op = pb("op", [P, 2, D])

        s_const = sem("s_const")
        s_gatehi = sem("s_gatehi")
        s_passed_dve = sem("s_passed_dve")
        s_passed_pool = sem("s_passed_pool")
        s_tab = sem("s_tab")
        s_stage = [sem(f"s_stage{i}") for i in range(2)]
        s_split_hi = sem("s_split_hi")
        s_split_lo = sem("s_split_lo")
        s_wstore = [sem(f"s_wstore{i}") for i in range(2)]
        s_estore = sem("s_estore")
        s_wload = sem("s_wload")
        s_idx = sem("s_idx")
        s_gather = sem("s_gather")
        s_loraT = sem("s_loraT")
        s_loraC = sem("s_loraC")
        s_loraM = sem("s_loraM")
        s_emb = sem("s_emb")
        s_stat = sem("s_stat")
        s_aggr = sem("s_aggr")
        s_var = sem("s_var")
        s_std = sem("s_std")
        s_rstd = sem("s_rstd")
        s_xn = sem("s_xn")
        s_xt = sem("s_xt")
        s_xh = sem("s_xh")
        s_xl = sem("s_xl")
        s_pj = sem("s_pj")
        s_sq = sem("s_sq")
        s_vraw = sem("s_vraw")
        s_rope = sem("s_rope")
        s_radd = sem("s_radd")
        s_root = sem("s_root")
        s_rms = sem("s_rms")
        s_rinv = sem("s_rinv")
        s_qkn = sem("s_qkn")
        s_qkT = sem("s_qkT")
        s_qkh = sem("s_qkh")
        s_qkl = sem("s_qkl")
        s_vh = sem("s_vh")
        s_vl = sem("s_vl")
        s_score = sem("s_score")
        s_bias = sem("s_bias")
        s_exp = sem("s_exp")
        s_rsum = sem("s_rsum")
        s_prob = sem("s_prob")
        s_prob_late = sem("s_prob_late")
        s_pT = sem("s_pT")
        s_pTh = sem("s_pTh")
        s_pTl = sem("s_pTl")
        s_pv = sem("s_pv")
        s_yh = sem("s_yh")
        s_yl = sem("s_yl")
        s_op = sem("s_op")
        s_hadd = sem("s_hadd")
        s_gate = sem("s_gate")
        s_rt = sem("s_rt")
        s_rw = sem("s_rw")
        s_gdiff = sem("s_gdiff")
        s_gexp = sem("s_gexp")
        s_ff = sem("s_ff")
        s_ffc = sem("s_ffc")
        s_stored = sem("s_stored")

        TABS = 3 * NT + 2
        CONSTS = 8

        block = ctx.enter_context(nc.Block())

        WO_PIECES = 4
        EARLY = 2 + WO_PIECES + NKV - 2
        PIECES = EARLY + NCH

        def staged(i):
            if i < EARLY:
                return prob[:, 2 * (i % 2):2 * (i % 2) + 2, :].rearrange("p a n -> p (a n)")
            if i % 2 == 0:
                return h[:, 1].rearrange("p t d -> p (t d)")
            return emb[:].rearrange("p t d -> p (t d)")[:, 0:SL]

        def parts(i):
            if i < 2:
                return W[:, i].rearrange("p a k n -> p a (k n)")
            if i < 2 + WO_PIECES:
                return wo_s[:, :, 4 * (i - 2):4 * (i - 2) + 4, :].rearrange("p a k n -> p a (k n)")
            if i < EARLY:
                return pT[:, 0, i % 2].rearrange("p (a k) n -> p a (k n)", a=2)
            return lnT[1][:].rearrange("p a k n -> p a (k n)")

        def slice_of(i):
            return i if i < 2 else None if i < 2 + WO_PIECES else i - WO_PIECES

        def ahead(u):
            return [u + 2] if u < 4 else [6, 7] if u == 4 else []

        @block.sync
        def _(sp):
            for dst, src in ((ident_f[:], ident), (norm_in[:], norm_w), (cs[:], rope),
                             (iota_e[:], iota), (loraB[:], lora_b), (gate_f[:], gate), (mask_f[:], mask),
                             (idx_all[:], ids)):
                sp.dma_start(dst, src).then_inc(s_const, 16)

            def stage(i):
                src = w_slices[slice_of(i)] if slice_of(i) is not None else wo[:, (i - 2) * SL:(i - 1) * SL]
                sp.dma_start(staged(i), src).then_inc(s_stage[i % 2], 16)

            def store_parts(i):
                sp.wait_ge(s_split_hi, i + 1)
                sp.wait_ge(s_split_lo, i + 1)
                if slice_of(i) is not None:
                    sp.dma_start(w_split[slice_of(i)], parts(i).rearrange("p a n -> p (a n)").bitcast(F32))\
                        .then_inc(s_wstore[i % 2] if i < EARLY else s_estore, 16)

            stage(0)
            stage(1)
            for i in range(EARLY):
                store_parts(i)
                if i + 2 < EARLY:
                    stage(i + 2)

            def load(s, before):
                wait_past(sp, s_wload, 16 * before)
                sp.dma_start(W[:, s % 2].rearrange("p a k n -> p (a k n)").bitcast(F32), w_split[s])\
                    .then_inc(s_wload, 16)

            def store(b):
                sp.wait_ge(s_ffc, 2 * 16 * (b + 1) + 1)
                sp.dma_start(out[bass.ds(b, 1)].rearrange("a (t p) d -> p (a t) d", p=P),
                             h[:, bass.ds(b % 2, 1)].rearrange("p a t d -> p (a t) d"))\
                    .then_inc(s_stored, 16)

            def sequence(b, first, last):
                done = NS * b + (1 if first else 0)
                for s in range(3 if first else 2, NKV):
                    if s > 3 or first:
                        sp.wait_ge(s_pj, NT * (NKV * b + s - 1))
                    else:
                        sp.wait_ge(s_ff, 16 * b - NT * (3 - s))
                    load(s, done)
                    done = done + 1
                    if s == 3 and not first:
                        store(b - 1)
                if not last:
                    for s in range(2):
                        sp.wait_ge(s_pj, NT * (NKV * b + NKV - 1 + s))
                        load(s, done)
                        done = done + 1
                for c in range(NCH):
                    if c < 2:
                        sp.wait_ge(s_pj, NT * (NKV * b + NKV + c + (-1 if last else 1)))
                    else:
                        sp.wait_ge(s_ff, 16 * b + NT * (c - 1))
                    load(NKV + c, done)
                    done = done + 1

            for k in range(2):
                sp.wait_ge(s_wstore[k], 16 * (NKV // 2))
            sp.wait_ge(s_pj, NT)
            load(2, 0)
            stage(EARLY)
            sp.wait_ge(s_emb, 2)
            stage(EARLY + 1)
            for i in range(EARLY, PIECES):
                store_parts(i)
                if i + 2 < PIECES:
                    stage(i + 2)
            sp.wait_ge(s_estore, 16 * NCH)
            sequence(0, True, False)
            with sp.Fori(1, B - 1) as b:
                sequence(b, False, False)
            sequence(B - 1, False, True)
            store(B - 1)
            sp.wait_ge(s_stored, 16 * (B + 1))

        def expert_load(b, c, last):
            return 16 * (NS * b + NKV + c + (-1 if last else 1))

        @block.gpsimd
        def _(pool):
            nc.gpsimd.memset(half[:], 0.5).then_inc(s_stored, 16)

            def fetch(b):
                nc.gpsimd.tensor_copy(idx_cur[:], idx_all[:, bass.ds(b * NT, NT)]).then_inc(s_idx, 1)
                pool.wait_ge(s_idx, b + 1)
                stand_alone(pool, s_passed_pool)
                for t in range(NT):
                    nc.gpsimd.indirect_dma_start(
                        out=emb[:, t, :], out_offset=None, in_=table,
                        in_offset=bass.IndirectOffsetOnAxis(ap=idx_cur[:, t:t + 1], axis=0))\
                        .then_inc(s_gather, 16)

            def norm_root(e):
                pool.wait_ge(s_aggr, NT * (e + 1))
                stand_alone(pool, s_passed_pool)
                nc.gpsimd.tensor_scalar(std[:], mv[:, :, 1], LN_EPS, 1.0, ALU.add, ALU.mult)\
                    .then_inc(s_var, 1)
                pool.wait_ge(s_var, e + 1)
                nc.gpsimd.tensor_tensor(std[:], std[:], half[:, 0:NT], ALU.pow).then_inc(s_std, 1)

            def rotate_sum(n, t):
                pool.wait_ge(s_rope, NT * n + t + 1)
                nc.gpsimd.tensor_tensor(ropeA[:, t], ropeA[:, t], ropeB[:, t], ALU.add)\
                    .then_inc(s_radd, 1)

            def head_rms(n, pair):
                def rows(x):
                    return x[:, 2 * pair:2 * pair + 2].rearrange("p t c -> p (t c)")

                pool.wait_ge(s_sq, 12 * n + 6 * (pair + 1))
                nc.gpsimd.tensor_tensor(rows(rms), rows(ssq), half[:, 0:6], ALU.pow).then_inc(s_root, 1)
                pool.wait_ge(s_root, 2 * n + pair + 1)
                stand_alone(pool, s_passed_pool)
                nc.gpsimd.tensor_scalar(rows(rms), rows(rms), RMS_EPS, 1.0, ALU.add, ALU.mult)\
                    .then_inc(s_rms, 1)

            def norm_heads(n, t):
                if t % 2 == 0:
                    pool.wait_ge(s_rinv, 2 * n + t // 2 + 1)
                pool.wait_ge(s_radd, NT * n + t + 1)
                nc.gpsimd.tensor_tensor(ropeA[:, t], ropeA[:, t],
                                        rinv[:, t][:, :, None].to_broadcast([P, 3, HD]), ALU.mult)\
                    .then_inc(s_qkn, 1)

            def normalise(n, u):
                pool.wait_ge(s_rsum, U * n + u + 1)
                stand_alone(pool, s_passed_pool)
                w = (u % NT + 1) * P
                nc.gpsimd.tensor_scalar(prob[:, u % 4, 0:w], prob[:, u % 4, 0:w], rsum[:, u:u + 1],
                                        1.0, ALU.mult, ALU.mult).then_inc(s_prob, 1)

            def group(n, nxt=True, norm=None):
                for u in range(U):
                    if u == 2 and nxt:
                        head_rms(n + 1, 0)
                    if u in (0, 1, 3) and nxt:
                        rotate_sum(n + 1, u)
                    if u + 2 < 6:
                        normalise(n, u + 2)
                    if u == 2 and nxt:
                        rotate_sum(n + 1, u)
                    if u == 3 and nxt:
                        norm_heads(n + 1, 0)
                        norm_heads(n + 1, 1)
                        head_rms(n + 1, 1)
                if norm is not None:
                    norm_root(norm)
                if nxt:
                    norm_heads(n + 1, 2)
                    norm_heads(n + 1, 3)
                    normalise(n + 1, 0)
                    normalise(n + 1, 1)

            pool.wait_ge(s_const, 16 * CONSTS)
            fetch(0)
            norm_root(0)
            for t in range(NT):
                rotate_sum(0, t)
            head_rms(0, 0)
            head_rms(0, 1)
            for t in range(NT):
                norm_heads(0, t)
            normalise(0, 0)
            normalise(0, 1)
            group(0)
            with pool.Fori(0, B - 1) as b:
                n = NKV * b
                pool.wait_ge(s_emb, 2 * (b + 1))
                pool.wait_ge(s_split_lo, PIECES)
                fetch(b + 1)
                with pool.Fori(1, NKV - 2) as g:
                    group(n + g)
                group(n + NKV - 2, norm=2 * b + 1)
                group(n + NKV - 1)
                group(n + NKV, norm=2 * b + 2)
            n = NKV * (B - 1)
            with pool.Fori(1, NKV - 1) as g:
                group(n + g)
            group(n + NKV - 1, nxt=False)
            norm_root(2 * B - 1)

        @block.scalar
        def _(act):
            copy = ACT.Copy

            def split(i):
                act.wait_ge(s_stage[i % 2], 16 * (i // 2 + 1))
                if 2 + WO_PIECES + 2 <= i < EARLY:
                    act.wait_ge(s_wstore[i % 2], 16 * ((i - WO_PIECES) // 2))
                if i > EARLY:
                    act.wait_ge(s_estore, 16 * (i - EARLY))
                nc.scalar.activation(parts(i)[:, 0], staged(i), copy).then_inc(s_split_hi, 1)

            act.wait_ge(s_const, 16 * CONSTS)
            nc.scalar.activation(gate_s[:, 0], gate_f[:], copy).then_inc(s_gatehi, 1)

            def lora_copy(b):
                act.wait_ge(s_loraT, b + 1)
                nc.scalar.activation(loraT[:], ov[0:R, :], copy).then_inc(s_loraC, 1)

            def normed_hi(e, which, tiles=range(NT)):
                for t in tiles:
                    act.wait_ge(s_xt, NT * e + t + 1)
                    nc.scalar.activation(lnT[which][:, 0, :, t * P:(t + 1) * P], tp[t % 2][:, 0:KC, :],
                                         copy).then_inc(s_xh, 1)

            def squares(n, t):
                act.wait_ge(s_pj, NT * n + t + 1)
                for c in range(3):
                    wait_past(act, s_sq, 12 * n + 3 * t + c - 3)
                    nc.scalar.activation(sq_junk[:, (3 * t + c) % 4], pj[t % 2][:, c * HD:(c + 1) * HD],
                                         ACT.Square, scale=float(HD) ** -0.5,
                                         accum_out=ssq[:, t, c:c + 1]).then_inc(s_sq, 1)
                if t == 0:
                    wait_past(act, s_vl, n)
                nc.scalar.activation(vraw[:, t], pj[t % 2][:, 3 * HD:], copy).then_inc(s_vraw, 1)

            def queries_hi(n, t):
                act.wait_ge(s_qkT, NT * n + t + 1)
                nc.scalar.activation(qkT[:, 0, :, t * P:(t + 1) * P], tp[t % 2][:, 0:3, :], copy)\
                    .then_inc(s_qkh, 1)

            def values_hi(n):
                act.wait_ge(s_vraw, NT * (n + 1))
                nc.scalar.activation(V[:, 0], vraw[:], copy).then_inc(s_vh, 1)

            def exponential(n, u):
                act.wait_ge(s_bias, U * n + u + 1)
                w = (u % NT + 1) * P
                nc.scalar.activation(prob[:, u % 4, 0:w], sc[u % 2][:, 0:w], ACT.Exp,
                                     bias=nbias[:, u:u + 1],
                                     accum_out=rowsum[:, u:u + 1]).then_inc(s_exp, 1)

            def normalise(n, u):
                act.wait_ge(s_rsum, U * n + u + 1)
                w = (u % NT + 1) * P
                nc.scalar.activation(prob[:, u % 4, 0:w], prob[:, u % 4, 0:w], copy,
                                     scale=rsum[:, u:u + 1]).then_inc(s_prob_late, 1)

            def probs_hi(n, u):
                act.wait_ge(s_pT, U * n + u + 1)
                t = u % NT
                nc.scalar.activation(pT[:, u // NT, 0, 0:t + 1, t * P:(t + 1) * P],
                                     tp[u % 2][:, 0:t + 1, :], copy).then_inc(s_pTh, 1)

            def heads_hi(n, r):
                act.wait_ge(s_pv, REP * n + r + 1)
                nc.scalar.activation(yT[:, r, 0], ov[:], copy).then_inc(s_yh, 1)

            def expert_odds(b):
                act.wait_ge(s_gdiff, b + 1)
                nc.scalar.activation(gexp[:], gdiff[:], ACT.Exp).then_inc(s_gexp, 1)

            def group(n, carry=True, nxt=True, embed=None, finish=None):
                def norm_hi(t):
                    if embed is not None:
                        normed_hi(2 * embed - 1, 0, [t])
                    if finish is not None:
                        normed_hi(2 * finish + 2, 1, [t])

                for u in range(U):
                    if u == 0 and embed is not None:
                        lora_copy(embed)
                    if u < NT and nxt:
                        squares(n + 1, u)
                    if u == 6:
                        normalise(n, 7)
                        if nxt:
                            queries_hi(n + 1, 1)
                    if isinstance(n, int) and n == 0 and u % 2 == 0:
                        split(EARLY + u // 2)
                    probs_hi(n, u)
                    if u == 5:
                        normalise(n, 6)
                    if u == 5 and nxt:
                        queries_hi(n + 1, 0)
                    for v in ahead(u):
                        exponential(n, v)
                if carry:
                    act.wait_ge(s_op, 2 * n)
                heads_hi(n, 0)
                if nxt:
                    exponential(n + 1, 0)
                    exponential(n + 1, 1)
                    queries_hi(n + 1, 2)
                    queries_hi(n + 1, 3)
                heads_hi(n, 1)
                for t in range(NT):
                    norm_hi(t)
                if nxt:
                    values_hi(n + 1)
                if finish is not None:
                    expert_odds(finish)

            split(0)
            split(1)
            lora_copy(0)
            split(2)
            split(3)
            normed_hi(0, 0)
            split(4)
            for t in range(NT):
                squares(0, t)
            split(5)
            values_hi(0)
            split(6)
            queries_hi(0, 0)
            queries_hi(0, 1)
            split(7)
            queries_hi(0, 2)
            queries_hi(0, 3)
            for i in range(8, EARLY):
                split(i)
            exponential(0, 0)
            exponential(0, 1)
            for k in range(2):
                act.wait_ge(s_wstore[k], 16 * (NKV // 2))
            group(0, carry=False)
            act.wait_ge(s_estore, 16 * NCH)
            with act.Fori(0, B - 1) as b:
                n = NKV * b
                with act.Fori(1, NKV - 2) as g:
                    group(n + g)
                group(n + NKV - 2, embed=b + 1)
                group(n + NKV - 1)
                group(n + NKV, carry=False, finish=b)
            n = NKV * (B - 1)
            with act.Fori(1, NKV - 1) as g:
                group(n + g)
            group(n + NKV - 1, nxt=False)
            normed_hi(2 * B - 1, 1)
            expert_odds(B - 1)

        @block.vector
        def _(dve):
            def raw(x):
                return x.bitcast(F32)

            dve.wait_ge(s_const, 16 * CONSTS)
            nc.vector.tensor_scalar(norm_in[:, 0], norm_in[:, 0], ATT_SCALE, None, ALU.mult)\
                .then_inc(s_tab, 1)
            dve.wait_ge(s_tab, 1)
            for c in range(3):
                wsel = norm_in[:, 0 if c < 2 else 1]
                for t in range(NT):
                    nc.vector.tensor_tensor(tabA[:, t, c].rearrange("p (a d) -> p a d", a=2), wsel,
                                            cs[:, 0, t][:, None, :].to_broadcast([P, 2, HD // 2]),
                                            ALU.mult)
                    nc.vector.tensor_tensor(tabB[:, t, c, HD // 2:], wsel[:, 0], cs[:, 1, t], ALU.mult)
                    nc.vector.scalar_tensor_tensor(tabB[:, t, c, 0:HD // 2], wsel[:, 1], -1.0,
                                                   cs[:, 1, t], ALU.mult, ALU.mult).then_inc(s_tab, 1)
            nc.vector.tensor_copy(ident_b[:], ident_f[:])
            nc.vector.tensor_copy(mask_b[:], mask_f[:]).then_inc(s_tab, 1)
            dve.wait_ge(s_tab, TABS)
            dve.wait_ge(s_gatehi, 1)
            nc.vector.tensor_tensor(gate_s[:, 1], gate_f[:], raw(gate_s[:, 0]), ALU.subtract)\
                .then_inc(s_tab, 1)

            def split(i):
                dve.wait_ge(s_split_hi, i + 1)
                nc.vector.tensor_tensor(parts(i)[:, 1], staged(i), raw(parts(i)[:, 0]), ALU.subtract)\
                    .then_inc(s_split_lo, 1)

            def embed(b, pairs=range(2)):
                wait_past(dve, s_stored, 16 * b)
                for pair in pairs:
                    dve.wait_ge(s_loraM, 2 * b + pair + 1)
                    bank = op[:] if pair == 0 else ov[:].rearrange("p (t d) -> p t d", t=2)
                    nc.vector.scalar_tensor_tensor(
                        h[:, bass.ds(b % 2, 1), 2 * pair:2 * pair + 2].rearrange("p a t d -> p (a t) d"),
                        bank, LORA_SCALING, emb[:, 2 * pair:2 * pair + 2, 0:D], ALU.mult, ALU.add)\
                        .then_inc(s_emb, 1)

            def h_tile(b, t):
                return h[:, bass.ds(b % 2, 1), t].rearrange("p a d -> p (a d)")

            def norm_stats(e, b):
                stand_alone(dve, s_passed_dve)
                for t in range(NT):
                    nc.vector.bn_stats(stats[:, t], h_tile(b, t)).then_inc(s_stat, 1)
                for t in range(NT):
                    dve.wait_ge(s_stat, NT * e + t + 1)
                    stand_alone(dve, s_passed_dve)
                    nc.vector.bn_aggr(mv[:, t], stats[:, t]).then_inc(s_aggr, 1)

            def norm_apply(e, b, tiles=range(NT)):
                if 0 in tiles:
                    dve.wait_ge(s_std, e + 1)
                    nc.vector.reciprocal(rstd[:], std[:]).then_inc(s_rstd, 1)
                    dve.wait_ge(s_rstd, e + 1)
                for t in tiles:
                    nc.vector.tensor_scalar(xn[:, t], h_tile(b, t), mv[:, t, 0:1], rstd[:, t:t + 1],
                                            ALU.subtract, ALU.mult).then_inc(s_xn, 1)

            def normed_lo(e, which, tiles=range(NT)):
                for t in tiles:
                    dve.wait_ge(s_xh, NT * e + t + 1)
                    cols = slice(t * P, (t + 1) * P)
                    nc.vector.tensor_tensor(lnT[which][:, 1, :, cols], tp[t % 2][:, 0:KC, :],
                                            raw(lnT[which][:, 0, :, cols]), ALU.subtract)\
                        .then_inc(s_xl, 1)

            def rotate(n, t):
                dve.wait_ge(s_vraw, NT * n + t + 1)
                wait_past(dve, s_qkT, NT * (n - 1) + t + 1)
                qk = pj[t % 2][:, 0:3 * HD]
                nc.vector.tensor_tensor(ropeA[:, t], qk.rearrange("p (c d) -> p c d", c=3), tabA[:, t],
                                        ALU.mult)
                nc.vector.tensor_tensor(
                    ropeB[:, t].rearrange("p c (a d) -> p c a d", a=2),
                    qk.rearrange("p (c a d) -> p c a d", c=3, a=2)[:, :, ::-1, :],
                    tabB[:, t].rearrange("p c (a d) -> p c a d", a=2), ALU.mult).then_inc(s_rope, 1)

            def norm_factors(n, pair):
                dve.wait_ge(s_rms, 2 * n + pair + 1)
                nc.vector.reciprocal(rinv[:, 2 * pair:2 * pair + 2], rms[:, 2 * pair:2 * pair + 2])\
                    .then_inc(s_rinv, 1)

            def queries_lo(n, t):
                dve.wait_ge(s_qkh, NT * n + t + 1)
                cols = slice(t * P, (t + 1) * P)
                nc.vector.tensor_tensor(qkT[:, 1, :, cols], tp[t % 2][:, 0:3, :],
                                        raw(qkT[:, 0, :, cols]), ALU.subtract).then_inc(s_qkl, 1)

            def values_lo(n):
                dve.wait_ge(s_vh, n + 1)
                nc.vector.tensor_tensor(V[:, 1], vraw[:], raw(V[:, 0]), ALU.subtract).then_inc(s_vl, 1)

            def maximum(n, u):
                dve.wait_ge(s_score, U * n + u + 1)
                nc.vector.tensor_reduce(nbias[:, u:u + 1], sc[u % 2][:, 0:(u % NT + 1) * P], AX,
                                        ALU.max, negate=True).then_inc(s_bias, 1)

            def inverse_sum(n, u):
                dve.wait_ge(s_exp, U * n + u + 1)
                nc.vector.reciprocal(rsum[:, u:u + 1], rowsum[:, u:u + 1]).then_inc(s_rsum, 1)

            def probs_lo(n, u):
                dve.wait_ge(s_pTh, U * n + u + 1)
                r, t = u // NT, u % NT
                cols = slice(t * P, (t + 1) * P)
                nc.vector.tensor_tensor(pT[:, r, 1, 0:t + 1, cols], tp[u % 2][:, 0:t + 1, :],
                                        raw(pT[:, r, 0, 0:t + 1, cols]), ALU.subtract)\
                    .then_inc(s_pTl, 1)

            def heads_lo(n, r):
                dve.wait_ge(s_yh, REP * n + r + 1)
                nc.vector.tensor_tensor(yT[:, r, 1], ov[:], raw(yT[:, r, 0]), ALU.subtract)\
                    .then_inc(s_yl, 1)

            def add_attention(n, b, pair):
                dve.wait_ge(s_op, 2 * n + pair + 1)
                dst = h[:, bass.ds(b % 2, 1), 2 * pair:2 * pair + 2].rearrange("p a t d -> p (a t) d")
                nc.vector.tensor_tensor(dst, op[:], dst, ALU.add).then_inc(s_hadd, 1)

            def router(b):
                k = [6 * b]

                def step(ins):
                    k[0] = k[0] + 1
                    ins.then_inc(s_rt, 1)
                    dve.wait_ge(s_rt, k[0])

                dve.wait_ge(s_gate, b + 1)
                step(nc.vector.tensor_copy(logits[:].rearrange("p t e -> p (t e)"), op[:, 0, 0:NT * NE]))
                stand_alone(dve, s_passed_dve)
                for t in range(NT):
                    last = nc.vector.max(top8[:, t], logits[:, t])
                step(last)
                nc.vector.tensor_tensor(gdiff[:], top8[:, :, 1], top8[:, :, 0], ALU.subtract)\
                    .then_inc(s_gdiff, 1)
                stand_alone(dve, s_passed_dve)
                for t in range(NT):
                    last = nc.vector.max_index(top8i[:, t], top8[:, t], logits[:, t])
                step(last)
                step(nc.vector.tensor_copy(topf[:], top8i[:, :, 0:2]))
                for i in range(2):
                    nc.vector.tensor_tensor(hot[:, i], iota_e[:][:, None, :].to_broadcast([P, NT, NE]),
                                            topf[:, :, i:i + 1].to_broadcast([P, NT, NE]), ALU.is_equal)
                dve.wait_ge(s_gexp, b + 1)
                step(nc.vector.tensor_scalar(gden[:], gexp[:], 1.0, None, ALU.add))
                step(nc.vector.reciprocal(gw[:, 0], gden[:]))

            def router_weights(b):
                k = 3 * b
                nc.vector.tensor_tensor(gw[:, 1], gw[:, 0], gexp[:], ALU.mult).then_inc(s_rw, 1)
                dve.wait_ge(s_rw, k + 1)
                for i in range(2):
                    last = nc.vector.tensor_tensor(hot[:, i], hot[:, i],
                                                   gw[:, i][:, :, None].to_broadcast([P, NT, NE]), ALU.mult)
                last.then_inc(s_rw, 1)
                dve.wait_ge(s_rw, k + 2)
                nc.vector.tensor_tensor(wfull[:], hot[:, 0], hot[:, 1], ALU.add).then_inc(s_rw, 1)
                dve.wait_ge(s_rw, k + 3)

            def experts(b):
                for f in range(NCH * NT):
                    c, t = divmod(f, NT)
                    dve.wait_ge(s_ff, 16 * b + f + 1)
                    for i in range(EPC):
                        if i:
                            dve.wait_ge(s_ffc, 32 * b + 2 * f + 2)
                        e = EPC * c + i
                        nc.vector.scalar_tensor_tensor(h_tile(b, t), pj[f % 2][:, i * D:(i + 1) * D],
                                                       wfull[:, t, e:e + 1], h_tile(b, t),
                                                       ALU.mult, ALU.add).then_inc(s_ffc, 1)

            def group(n, b, carry=True, nxt=True, embed_next=False, finish=None):
                norm = 2 * b + 1 if embed_next else 2 * finish + 2 if finish is not None else None
                nb = b + 1 if embed_next else finish

                def norm_lo(t):
                    if norm is not None:
                        normed_lo(norm, 0 if embed_next else 1, [t])

                for u in range(U):
                    if u in (2, 4) and finish is not None:
                        add_attention(n - 1, finish, u // 2 - 1)
                    if u == 5:
                        inverse_sum(n, 7)
                        probs_lo(n, u)
                    for v in ahead(u):
                        maximum(n, v)
                    if u < 2 and nxt:
                        rotate(n + 1, u)
                    if u == 6 and nxt:
                        norm_factors(n + 1, 1)
                        queries_lo(n + 1, 1)
                    if u != 5:
                        probs_lo(n, u)
                    if u == 4 and carry:
                        add_attention(n - 1, b, 0)
                    if isinstance(n, int) and n == 0 and u % 2 == 0:
                        split(EARLY + u // 2)
                    if 2 <= u < NT and nxt:
                        rotate(n + 1, u)
                    if u == 5 and nxt:
                        queries_lo(n + 1, 0)
                    if u + 2 < 7:
                        inverse_sum(n, u + 2)
                    if u == 3 and nxt:
                        norm_factors(n + 1, 0)
                    if u in (1, 2) and embed_next:
                        embed(nb, [u - 1])
                    if u == 4 and norm is not None:
                        if embed_next:
                            dve.wait_ge(s_emb, 2 * (nb + 1))
                        else:
                            dve.wait_ge(s_hadd, 1 + 2 * n)
                        norm_stats(norm, nb)
                if norm is not None:
                    norm_apply(norm, nb, range(2))
                heads_lo(n, 0)
                if nxt:
                    maximum(n + 1, 0)
                    maximum(n + 1, 1)
                if norm is not None:
                    norm_apply(norm, nb, range(2, NT))
                if carry:
                    add_attention(n - 1, b, 1)
                if nxt:
                    inverse_sum(n + 1, 0)
                    inverse_sum(n + 1, 1)
                    queries_lo(n + 1, 2)
                    queries_lo(n + 1, 3)
                heads_lo(n, 1)
                for t in range(NT):
                    norm_lo(t)
                if nxt:
                    values_lo(n + 1)
                if finish is not None:
                    router(finish)
                    router_weights(finish)
                    experts(finish)

            dve.sem_inc(s_hadd, 1)
            dve.sem_inc(s_ffc, 1)
            split(0)
            split(1)
            embed(0)
            dve.wait_ge(s_emb, 2)
            norm_stats(0, 0)
            split(2)
            split(3)
            norm_apply(0, 0)
            normed_lo(0, 0)
            split(4)
            for t in range(NT):
                rotate(0, t)
            split(5)
            for pair in range(2):
                norm_factors(0, pair)
            values_lo(0)
            split(6)
            queries_lo(0, 0)
            queries_lo(0, 1)
            split(7)
            queries_lo(0, 2)
            queries_lo(0, 3)
            for i in range(8, EARLY):
                split(i)
            maximum(0, 0)
            maximum(0, 1)
            inverse_sum(0, 0)
            inverse_sum(0, 1)
            group(0, 0, carry=False)
            with dve.Fori(0, B - 1) as b:
                n = NKV * b
                with dve.Fori(1, NKV - 2) as g:
                    group(n + g, b)
                group(n + NKV - 2, b, embed_next=True)
                group(n + NKV - 1, b)
                group(n + NKV, b + 1, carry=False, finish=b)
            b = B - 1
            n = NKV * b
            with dve.Fori(1, NKV - 1) as g:
                group(n + g, b)
            n = n + NKV - 1
            group(n, b, nxt=False)
            for pair in range(2):
                add_attention(n, b, pair)
            dve.wait_ge(s_hadd, 1 + 2 * (n + 1))
            norm_stats(2 * B - 1, b)
            norm_apply(2 * B - 1, b)
            normed_lo(2 * B - 1, 1)
            router(b)
            router_weights(b)
            experts(b)

        @block.tensor
        def _(pe):
            mm = nc.tensor.matmul

            def three_pass(dst, lhs, rhs, start, stop):
                mm(dst, lhs[0], rhs[0], start=start, stop=False)
                mm(dst, lhs[0], rhs[1], start=False, stop=False)
                return mm(dst, lhs[1], rhs[0], start=False, stop=stop)

            def lora_transpose(b, n):
                pe.wait_ge(s_gather, 64 * (b + 1))
                wait_past(pe, s_yl, REP * n)
                for t in range(NT):
                    last = nc.tensor.transpose(ov[0:R, t * P:(t + 1) * P], emb[:, t, D:D + R], ident_f[:])
                last.then_inc(s_loraT, 1)

            def lora_product(b, n):
                pe.wait_ge(s_loraC, b + 1)
                wait_past(pe, s_hadd, 2 * n - 1)
                for pair in range(2):
                    bank = op[:] if pair == 0 else ov[:].rearrange("p (t d) -> p t d", t=2)
                    for i in range(2):
                        t = 2 * pair + i
                        last = mm(bank[:, i], loraT[:, t * P:(t + 1) * P], loraB[:], start=True, stop=True)
                    last.then_inc(s_loraM, 1)

            def norm_transpose(e, t, before=None):
                pe.wait_ge(s_xn, NT * e + t + 1)
                if before is not None:
                    pe.wait_ge(*before)
                elif t >= 2:
                    pe.wait_ge(s_xl, NT * e + t - 1)
                for k in range(KC):
                    last = nc.tensor.transpose(tp[t % 2][:, k], xn[:, t, k * P:(k + 1) * P], ident_f[:])
                last.then_inc(s_xt, 1)

            def project(n, t, slot, bank_free):
                for s, v in bank_free:
                    wait_past(pe, s, v)
                for k in range(KC):
                    last = three_pass(pj[t % 2][:], [lnT[0][:, x, k, t * P:(t + 1) * P] for x in range(2)],
                                      [W[:, bass.ds(slot, 1), x, k, :].rearrange("p a n -> p (a n)")
                                       for x in range(2)], start=k == 0, stop=k == KC - 1)
                last.then_inc(s_pj, 1)

            def bank_read(n, t):
                return [(s_rope, NT * n + t + 1), (s_vraw, NT * n + t + 1)]

            def qk_transpose(n, t, before):
                pe.wait_ge(s_qkn, NT * n + t + 1)
                wait_past(pe, *before)
                for c in range(3):
                    last = nc.tensor.transpose(tp[t % 2][:, c], ropeA[:, t, c], ident_f[:])
                last.then_inc(s_qkT, 1)

            def score(n, u):
                r, t = u // NT, u % NT
                pe.wait_ge(s_qkl, NT * n + t + 1)
                w = (t + 1) * P
                if u >= 2:
                    pe.wait_ge(s_exp, U * n + u - 1)
                else:
                    wait_past(pe, s_exp, U * (n - 1) + u + 7)
                three_pass(sc[u % 2][:, 0:w], [qkT[:, x, r, t * P:(t + 1) * P] for x in range(2)],
                           [qkT[:, x, 2, 0:w] for x in range(2)], start=True, stop=False)
                mm(sc[u % 2][:, t * P:w], ident_b[:], mask_b[:], start=False, stop=True)\
                    .then_inc(s_score, 1)

            def prob_transpose(n, u, before):
                if u < 6:
                    pe.wait_ge(s_prob, 6 * n + u + 1)
                else:
                    pe.wait_ge(s_prob_late, 2 * n + u - 5)
                wait_past(pe, *before)
                for kt in range(u % NT + 1):
                    last = nc.tensor.transpose(tp[u % 2][:, kt], prob[:, u % 4, kt * P:(kt + 1) * P],
                                               ident_f[:])
                last.then_inc(s_pT, 1)

            def value_product(n, r):
                pe.wait_ge(s_pTl, U * n + NT * (r + 1))
                if r == 0:
                    pe.wait_ge(s_vl, n + 1)
                else:
                    pe.wait_ge(s_yl, REP * n + r)
                for kt in range(NT):
                    last = three_pass(ov[:, kt * P:], [V[:, x, kt] for x in range(2)],
                                      [pT[:, r, x, kt, kt * P:] for x in range(2)],
                                      start=kt == 0, stop=kt == NT - 1)
                last.then_inc(s_pv, 1)

            def output_product(n, g, pair, tiles=range(2)):
                if 0 in tiles:
                    pe.wait_ge(s_yl, REP * (n + 1))
                    pe.wait_ge(s_hadd, 2 * n + 1 + pair)
                for i in tiles:
                    t = 2 * pair + i
                    for r in range(REP):
                        last = three_pass(
                            op[:, i], [yT[:, r, x, t * P:(t + 1) * P] for x in range(2)],
                            [wo_s[:, x, bass.ds(REP * g + r, 1), :].rearrange("p a d -> p (a d)")
                             for x in range(2)], start=r == 0, stop=r == REP - 1)
                if 1 in tiles:
                    last.then_inc(s_op, 1)

            def project_first(n, b, g):
                pe.wait_ge(s_wload, 16 * (NS * b + g))
                project(n, 0, (g + 1) % 2, bank_read(n - 1, 2))

            def group(n, b, g, carry=True, nxt=True, embed=None, finish=None, fresh=None,
                      after_experts=False, ahead_next=True):
                norm = 2 * embed - 1 if embed is not None else 2 * finish + 2 if finish is not None else None

                def unit_read(u):
                    return s_pTl, U * n + u + 1

                def keys_read(m, t):
                    return s_qkl, NT * m + t + 1

                def norm_read(e, t):
                    return s_xl, NT * e + t + 1

                for u in range(U):
                    if 1 <= u < NT and nxt:
                        if fresh is not None:
                            pe.wait_ge(*norm_read(fresh, u))
                        if after_experts and u == 1:
                            pe.wait_ge(s_ffc, 32 * b + 1)
                        project(n + 1, u, (g + 1) % 2,
                                bank_read(n, u + 2) if u < 2 else bank_read(n + 1, u - 2))
                    if embed is not None:
                        if u == 0:
                            lora_transpose(embed, n)
                        if u == 1:
                            lora_product(embed, n)
                    if finish is not None and u in (1, 3):
                        output_product(n - 1, NKV - 1, u // 2)
                    if carry and u == 4:
                        if embed is not None:
                            pe.wait_ge(s_emb, 2 * embed + 1)
                        output_product(n - 1, g - 1, 0)
                    if u == 5:
                        if embed is not None:
                            pe.wait_ge(s_emb, 2 * (embed + 1))
                        value_product(n, 0)
                    if u == 6:
                        for t in range(2):
                            if nxt:
                                qk_transpose(n + 1, t, unit_read(4 + t))
                            if carry:
                                output_product(n - 1, g - 1, 1, [t])
                    if u < 2:
                        if fresh is not None:
                            pe.wait_ge(*norm_read(fresh, u + 2))
                        before = keys_read(n, u + 2)
                    elif u < 6 or not nxt:
                        before = unit_read(u - 2)
                    else:
                        before = keys_read(n + 1, u - 6)
                    if u == 4:
                        score(n, 6)
                    prob_transpose(n, u, before)
                    if u <= 4:
                        score(n, ahead(u)[-1])
                if nxt:
                    for t in range(2):
                        score(n + 1, t)
                    for t in range(2, NT):
                        qk_transpose(n + 1, t, unit_read(4 + t))
                        if t == 2 and ahead_next and norm is None:
                            project_first(n + 2, b, g + 1)
                value_product(n, 1)
                if norm is not None:
                    for t in range(NT):
                        norm_transpose(norm, t, keys_read(n + 1, 2 + t) if t < 2 else None)
                    if ahead_next:
                        pe.wait_ge(*norm_read(norm, 0))
                        project_first(n + 2, b, g + 1)
                if finish is not None:
                    router_product(norm)

            def router_product(e):
                pe.wait_ge(s_xl, NT * (e + 1))
                for t in range(NT):
                    for k in range(KC):
                        last = three_pass(op[:, 0, t * NE:(t + 1) * NE],
                                          [lnT[1][:, x, k, t * P:(t + 1) * P] for x in range(2)],
                                          [gate_s[:, x, k * NE:(k + 1) * NE] for x in range(2)],
                                          start=k == 0, stop=k == KC - 1)
                last.then_inc(s_gate, 1)

            def experts(b, n, last):
                for f in range(NCH * NT):
                    c, t = divmod(f, NT)
                    if t == 0:
                        pe.wait_ge(s_wload, expert_load(b, c, last))
                    if f < 2:
                        for s, v in bank_read(n, f + 2):
                            pe.wait_ge(s, v)
                    else:
                        pe.wait_ge(s_ffc, 32 * b + 2 * (f - 1) + 1)
                    for k in range(KC):
                        last_mm = three_pass(pj[f % 2][:],
                                             [lnT[1][:, x, k, t * P:(t + 1) * P] for x in range(2)],
                                             [W[:, c % 2, x, k, :] for x in range(2)],
                                             start=k == 0, stop=k == KC - 1)
                    last_mm.then_inc(s_ff, 1)

            pe.wait_ge(s_const, 16 * CONSTS)
            pe.wait_ge(s_tab, TABS + 1)
            lora_transpose(0, 0)
            lora_product(0, 0)
            for t in range(NT):
                norm_transpose(0, t)
            pe.wait_ge(s_split_lo, 1)
            for t in range(NT):
                pe.wait_ge(s_xl, t + 1)
                project(0, t, 0, [] if t < 2 else bank_read(0, t - 2))
            for t in range(NT):
                qk_transpose(0, t, (s_xl, 3 + t) if t < 2 else (s_qkl, t - 1))
            score(0, 0)
            score(0, 1)
            pe.wait_ge(s_emb, 2)
            pe.wait_ge(s_split_lo, EARLY)
            project(1, 0, 1, bank_read(0, 2))
            group(0, 0, 0, carry=False)
            with pe.Fori(0, B - 1) as b:
                n = NKV * b
                with pe.Fori(1, NKV - 2) as g:
                    group(n + g, b, g, after_experts=True)
                group(n + NKV - 2, b, NKV - 2, embed=b + 1)
                group(n + NKV - 1, b, NKV - 1, fresh=2 * b + 1)
                group(n + NKV, b + 1, 0, carry=False, finish=b, ahead_next=False)
                experts(b, n + NKV + 1, False)
                pe.wait_ge(s_ffc, 32 * b + 31)
                project_first(n + NKV + 2, b + 1, 1)
            b = B - 1
            n = NKV * b
            with pe.Fori(1, NKV - 2) as g:
                group(n + g, b, g, after_experts=True)
            group(n + NKV - 2, b, NKV - 2, ahead_next=False)
            n = n + NKV - 1
            group(n, b, NKV - 1, nxt=False)
            for pair in range(2):
                output_product(n, NKV - 1, pair)
            for t in range(NT):
                norm_transpose(2 * B - 1, t, (s_pTl, U * n + 7 + t) if t < 2 else None)
            router_product(2 * B - 1)
            experts(b, n, True)


def kernel(**inputs):
    import numpy as np
    import concourse.bacc as bacc
    from concourse.bass_utils import run_bass_kernel_spmd

    def arr(name):
        return np.asarray(inputs[name])

    table = np.concatenate([arr("L0_tok_emb_weight"), arr("L0_tok_lora_A").T], axis=1)
    ids = np.ascontiguousarray(arr("x").reshape(B * NT, P).T)
    def halves(w):
        return w.reshape(w.shape[0], -1, HD // 2, 2).transpose(0, 1, 3, 2).reshape(w.shape[0], -1, HD)

    wq = halves(arr("L0_attn_wq")).reshape(D, NKV, REP * HD)
    wk = halves(arr("L0_attn_wk"))
    wv = arr("L0_attn_wv").reshape(D, NKV, HD)
    qkv = np.concatenate([wq, wk, wv], axis=2).transpose(1, 0, 2)
    ew = arr("L0_ffn_expert_w").reshape(NCH, EPC * D, D).transpose(0, 2, 1)
    w_slices = np.concatenate([qkv, ew]).reshape(NS, KC, P, 512).transpose(0, 2, 1, 3)
    wo = arr("L0_attn_wo").reshape(NH, HD, D).transpose(1, 0, 2).reshape(HD, NH * D)
    gate = arr("L0_ffn_gate_w").T.reshape(KC, P, NE).transpose(1, 0, 2).reshape(P, KC * NE)
    norms = np.stack([arr("L0_attn_q_norm_w"), arr("L0_attn_k_norm_w")]).reshape(2, HD // 2, 2)
    norms = np.broadcast_to(norms.transpose(0, 2, 1), (P, 2, 2, HD // 2))
    theta = np.float32(1e6) ** (np.float32(-2.0) * np.arange(HD // 2, dtype=np.float32) / np.float32(HD))
    angle = np.arange(T, dtype=np.float32)[:, None] * theta[None, :].astype(np.float32)
    rope = np.stack([np.cos(angle), np.sin(angle)]).astype(np.float32)
    rope = rope.reshape(2, NT, P, HD // 2).transpose(2, 0, 1, 3)
    mask = np.triu(np.full((P, P), -3e37, np.float32), k=1)
    data = {
        "ids": ids, "table": table, "lora_b": arr("L0_tok_lora_B").T,
        "w_slices": w_slices.reshape(NS, P, SL), "wo": wo, "gate": gate, "norm_w": norms, "rope": rope,
        "ident": np.eye(P, dtype=np.float32), "mask": mask,
        "iota": np.broadcast_to(np.arange(NE, dtype=np.float32), (P, NE)),
    }
    nc = bacc.Bacc("TRN2", target_bir_lowering=False, num_devices=1)
    arrays, args = {}, {}
    for name, a in data.items():
        a = np.ascontiguousarray(a)
        arrays[f"in_{name}"] = a
        args[name] = nc.dram_tensor(f"in_{name}", a.shape, mybir.dt.from_np(a.dtype),
                                    kind="ExternalInput").ap()
    args["out"] = nc.dram_tensor("out_h", (B, T, D), F32, kind="ExternalOutput").ap()
    build_tower(nc, **args)
    r = run_bass_kernel_spmd(nc, [arrays], core_ids=[0])
    return r.results[0]["out_h"]
```
